# Optimizing a Trainium2 kernel written in Bass

```python
import numpy as np
import jax
import jax.numpy as jnp

def _softmax(x, axis=-1):
    return jax.nn.softmax(x, axis=axis)

def _gelu(x):
    return jax.nn.gelu(x, approximate=True)

def _silu(x):
    return jax.nn.silu(x)

def _sigmoid(x):
    return jax.nn.sigmoid(x)

def _layernorm(x, axis=-1, eps=1e-05):
    m = jnp.mean(x, axis=axis, keepdims=True)
    v = jnp.var(x, axis=axis, keepdims=True)
    return (x - m) / jnp.sqrt(v + eps)

def _scatter_add(tgt, idx, src, axis=0):
    return tgt.at[idx].add(src)

def _segment_sum(src, seg, n):
    return jax.ops.segment_sum(src, seg, n)
kernel_name = 'mk_prb_d2_jaxref_r4_28a8d3'

def setup_inputs(seed: int=0):
    np.random.seed(seed)
    _w = jnp.asarray

    def _L0_attn_setup():
        import jax, jax.numpy as jnp
        import numpy as np
        NH, HS, K = (32, 512, 16)
        HD = HS // NH
        B, L = (4, 512)
        EPS = 1e-06

        def _ln(x, gamma, beta):
            mu = x.mean(-1, keepdims=True)
            var = x.var(-1, keepdims=True)
            return gamma * ((x - mu) / jnp.sqrt(var + EPS)) + beta

        def _ln_fused_l2_bwd(x, target, gamma, beta):
            D = x.shape[-1]
            mu = x.mean(-1, keepdims=True)
            std = jnp.sqrt(x.var(-1, keepdims=True) + EPS)
            xh = (x - mu) / std
            gxh = (gamma * xh + beta - target) * gamma
            return (D * gxh - gxh.sum(-1, keepdims=True) - xh * (gxh * xh).sum(-1, keepdims=True)) / (D * std)

        def _forward(hidden_states, q_w, k_w, v_w, o_w, W1, b1, ttt_norm_weight, ttt_norm_bias, ttt_lr_weight, ttt_lr_bias, learnable_token_idx, post_norm_weight, post_norm_bias):
            Bb, Ll, _ = hidden_states.shape
            NM = Ll // K

            def proj_heads(w):
                return (hidden_states @ w.T).reshape(Bb, Ll, NH, HD).transpose(0, 2, 1, 3)
            XQ = proj_heads(q_w).reshape(Bb, NH, NM, K, HD)
            XK = proj_heads(k_w).reshape(Bb, NH, NM, K, HD)
            XV = proj_heads(v_w).reshape(Bb, NH, NM, K, HD)
            X = hidden_states.reshape(Bb, NM, K, HS)
            ttt_lr = jnp.einsum('bnkc,hdc->bhnkd', X, ttt_lr_weight) + ttt_lr_bias.reshape(1, NH, 1, 1, 1)
            ttt_lr_eta = jax.nn.sigmoid(ttt_lr).transpose(0, 1, 2, 4, 3) / HD
            token_idx = jnp.clip(1.0 / jnp.arange(1, K + 1, dtype=jnp.float32) + learnable_token_idx, 0.0, None)
            eta = token_idx.reshape(1, 1, 1, K, 1) * ttt_lr_eta
            ln_w = ttt_norm_weight.reshape(NH, 1, HD)
            ln_b = ttt_norm_bias.reshape(NH, 1, HD)

            def step(carry, x):
                W1_s, b1_s = carry
                xq, xk, xv, eta_mb = x
                Z1 = xk @ W1_s + b1_s
                grad = _ln_fused_l2_bwd(Z1, xv - xk, ln_w, ln_b)
                Attn1 = jnp.tril(xq @ xk.swapaxes(-1, -2))
                b1_bar = b1_s - jnp.tril(eta_mb) @ grad
                Z1_bar = xq @ W1_s - eta_mb * Attn1 @ grad + b1_bar
                last_eta = eta_mb[:, :, -1, :, None]
                W1_new = W1_s - (last_eta * xk).swapaxes(-1, -2) @ grad
                b1_new = b1_s - jnp.sum(last_eta * grad, axis=-2, keepdims=True)
                out = xq + _ln(Z1_bar, ln_w, ln_b)
                return ((W1_new, b1_new), out)
            init = (jnp.tile(W1[None], (Bb, 1, 1, 1)), jnp.tile(b1[None], (Bb, 1, 1, 1)))
            xs = (XQ.transpose(2, 0, 1, 3, 4), XK.transpose(2, 0, 1, 3, 4), XV.transpose(2, 0, 1, 3, 4), eta.transpose(2, 0, 1, 3, 4))
            _, ys = jax.lax.scan(step, init, xs)
            out = ys.transpose(1, 0, 3, 2, 4).reshape(Bb, Ll, HS)
            out = _ln(out, post_norm_weight, post_norm_bias)
            return out @ o_w.T
        key = jax.random.key(seed)
        ks = jax.random.split(key, 8)
        s = 0.02
        return {'hidden_states': jax.random.normal(ks[0], (B, L, HS), jnp.float32), 'position_ids': jnp.tile(jnp.arange(L, dtype=jnp.int32)[None], (B, 1)), 'q_w': jax.random.normal(ks[1], (HS, HS), jnp.float32) * s, 'k_w': jax.random.normal(ks[2], (HS, HS), jnp.float32) * s, 'v_w': jax.random.normal(ks[3], (HS, HS), jnp.float32) * s, 'o_w': jax.random.normal(ks[4], (HS, HS), jnp.float32) * s, 'W1': jax.random.normal(ks[5], (NH, HD, HD), jnp.float32) * s, 'b1': jnp.zeros((NH, 1, HD), jnp.float32), 'ttt_norm_weight': jnp.ones((NH, HD), jnp.float32), 'ttt_norm_bias': jnp.zeros((NH, HD), jnp.float32), 'ttt_lr_weight': jax.random.normal(ks[6], (NH, 1, HS), jnp.float32) * s, 'ttt_lr_bias': jnp.zeros((NH, 1), jnp.float32), 'learnable_token_idx': jnp.zeros((K,), jnp.float32), 'post_norm_weight': jnp.ones((HS,), jnp.float32), 'post_norm_bias': jnp.zeros((HS,), jnp.float32)}
    _L0_attn_in = _L0_attn_setup()

    def _L0_ffn_setup():
        import jax, jax.numpy as jnp
        import numpy as np
        HIDDEN = 512
        INTER = 1408
        B, S = (2, 512)

        def _ternary(key, shape):
            return jax.random.randint(key, shape, -1, 2).astype(jnp.float32)
        key = jax.random.key(seed)
        ks = jax.random.split(key, 7)
        x = jax.random.normal(ks[0], (B, S, HIDDEN), dtype=jnp.float32)
        gate_w = _ternary(ks[1], (INTER, HIDDEN))
        up_w = _ternary(ks[2], (INTER, HIDDEN))
        down_w = _ternary(ks[3], (HIDDEN, INTER))
        gate_s = jax.random.uniform(ks[4], (INTER,), minval=0.01, maxval=0.1, dtype=jnp.float32)
        up_s = jax.random.uniform(ks[5], (INTER,), minval=0.01, maxval=0.1, dtype=jnp.float32)
        down_s = jax.random.uniform(ks[6], (HIDDEN,), minval=0.01, maxval=0.1, dtype=jnp.float32)
        return {'x': x, 'gate_w': gate_w, 'up_w': up_w, 'down_w': down_w, 'gate_s': gate_s, 'up_s': up_s, 'down_s': down_s}
    _L0_ffn_in = _L0_ffn_setup()

    def _L1_attn_setup():
        import jax, jax.numpy as jnp
        import numpy as np
        B, S = (1, 1024)
        HID, H, D = (512, 16, 128)
        KVC, QC, RD = (128, 384, 64)
        THETA = 10000.0

        def _mla_forward(hidden_states, W_DKV, b_DKV, W_UK, b_UK, W_UV, b_UV, W_DQ, b_DQ, W_UQ, b_UQ, W_QR, W_KR, W_O, b_O):
            b, s, _ = hidden_states.shape
            c_kv = hidden_states @ W_DKV + b_DKV
            k = (c_kv @ W_UK + b_UK).reshape(b, s, H, D)
            v = (c_kv @ W_UV + b_UV).reshape(b, s, H, D)
            c_q = hidden_states @ W_DQ + b_DQ
            q = (c_q @ W_UQ + b_UQ).reshape(b, s, H, D)
            half = RD // 2
            inv_freq = 1.0 / THETA ** (jnp.arange(0, RD, 2, dtype=jnp.float32) / RD)
            t = jnp.arange(s, dtype=jnp.float32)
            freqs = t[:, None] * inv_freq[None, :]
            cos = jnp.cos(freqs)[None, :, None, :]
            sin = jnp.sin(freqs)[None, :, None, :]
            q_r = q @ W_QR
            k_r = k @ W_KR

            def rope(x):
                x1, x2 = (x[..., :half], x[..., half:])
                first = x1 * cos - x2 * sin
                return jnp.concatenate([first, jnp.zeros_like(first)], axis=-1)
            q = q.at[..., :RD].set(rope(q_r))
            k = k.at[..., :RD].set(rope(k_r))
            scores = jnp.einsum('bqhd,bkhd->bhqk', q, k) / jnp.sqrt(jnp.float32(D))
            probs = jax.nn.softmax(scores, axis=-1)
            ctx = jnp.einsum('bhqk,bkhd->bqhd', probs, v).reshape(b, s, H * D)
            return ctx @ W_O + b_O
        key = jax.random.key(seed)
        ks = jax.random.split(key, 16)
        w = lambda k, shp: jax.random.normal(k, shp, jnp.float32) * 0.02
        return {'hidden_states': jax.random.normal(ks[0], (B, S, HID), jnp.float32), 'W_DKV': w(ks[1], (HID, KVC)), 'b_DKV': jnp.zeros((KVC,), jnp.float32), 'W_UK': w(ks[2], (KVC, H * D)), 'b_UK': jnp.zeros((H * D,), jnp.float32), 'W_UV': w(ks[3], (KVC, H * D)), 'b_UV': jnp.zeros((H * D,), jnp.float32), 'W_DQ': w(ks[4], (HID, QC)), 'b_DQ': jnp.zeros((QC,), jnp.float32), 'W_UQ': w(ks[5], (QC, H * D)), 'b_UQ': jnp.zeros((H * D,), jnp.float32), 'W_QR': w(ks[6], (D, RD)), 'W_KR': w(ks[7], (D, RD)), 'W_O': w(ks[8], (H * D, HID)), 'b_O': jnp.zeros((HID,), jnp.float32)}
    _L1_attn_in = _L1_attn_setup()

    def _L1_ffn_setup():
        import jax, jax.numpy as jnp
        import numpy as np
        NUM_EXPERTS = 4
        key = jax.random.key(seed)
        k1, k2, k3 = jax.random.split(key, 3)
        B, N, H = (8, 512, 512)
        E = NUM_EXPERTS
        I = H * 4 // E
        x = jax.random.normal(k1, (B, N, H), dtype=jnp.float32)
        gate_up_proj = jax.random.normal(k2, (E, H, 2 * I), dtype=jnp.float32) * 0.02
        down_proj = jax.random.normal(k3, (E, I, H), dtype=jnp.float32) * 0.02
        return {'x': x, 'gate_up_proj': gate_up_proj, 'down_proj': down_proj}
    _L1_ffn_in = _L1_ffn_setup()
    _d = {'L0_attn_hidden_states': _L0_attn_in['hidden_states'], 'L0_attn_position_ids': _L0_attn_in['position_ids'], 'L0_attn_q_w': _L0_attn_in['q_w'], 'L0_attn_k_w': _L0_attn_in['k_w'], 'L0_attn_v_w': _L0_attn_in['v_w'], 'L0_attn_o_w': _L0_attn_in['o_w'], 'L0_attn_W1': _L0_attn_in['W1'], 'L0_attn_b1': _L0_attn_in['b1'], 'L0_attn_ttt_norm_weight': _L0_attn_in['ttt_norm_weight'], 'L0_attn_ttt_norm_bias': _L0_attn_in['ttt_norm_bias'], 'L0_attn_ttt_lr_weight': _L0_attn_in['ttt_lr_weight'], 'L0_attn_ttt_lr_bias': _L0_attn_in['ttt_lr_bias'], 'L0_attn_learnable_token_idx': _L0_attn_in['learnable_token_idx'], 'L0_attn_post_norm_weight': _L0_attn_in['post_norm_weight'], 'L0_attn_post_norm_bias': _L0_attn_in['post_norm_bias'], 'L0_ffn_gate_w': _L0_ffn_in['gate_w'], 'L0_ffn_up_w': _L0_ffn_in['up_w'], 'L0_ffn_down_w': _L0_ffn_in['down_w'], 'L0_ffn_gate_s': _L0_ffn_in['gate_s'], 'L0_ffn_up_s': _L0_ffn_in['up_s'], 'L0_ffn_down_s': _L0_ffn_in['down_s'], 'L1_attn_W_DKV': _L1_attn_in['W_DKV'], 'L1_attn_b_DKV': _L1_attn_in['b_DKV'], 'L1_attn_W_UK': _L1_attn_in['W_UK'], 'L1_attn_b_UK': _L1_attn_in['b_UK'], 'L1_attn_W_UV': _L1_attn_in['W_UV'], 'L1_attn_b_UV': _L1_attn_in['b_UV'], 'L1_attn_W_DQ': _L1_attn_in['W_DQ'], 'L1_attn_b_DQ': _L1_attn_in['b_DQ'], 'L1_attn_W_UQ': _L1_attn_in['W_UQ'], 'L1_attn_b_UQ': _L1_attn_in['b_UQ'], 'L1_attn_W_QR': _L1_attn_in['W_QR'], 'L1_attn_W_KR': _L1_attn_in['W_KR'], 'L1_attn_W_O': _L1_attn_in['W_O'], 'L1_attn_b_O': _L1_attn_in['b_O'], 'L1_ffn_gate_up_proj': _L1_ffn_in['gate_up_proj'], 'L1_ffn_down_proj': _L1_ffn_in['down_proj']}
    _x0 = _d['L0_attn_hidden_states']
    _d['L0_attn_hidden_states'] = jax.random.normal(jax.random.fold_in(jax.random.key(seed), 1), (4, 512, 512), dtype=_x0.dtype)
    del _x0
    return _d

def reference(L0_attn_hidden_states, L0_attn_position_ids, L0_attn_q_w, L0_attn_k_w, L0_attn_v_w, L0_attn_o_w, L0_attn_W1, L0_attn_b1, L0_attn_ttt_norm_weight, L0_attn_ttt_norm_bias, L0_attn_ttt_lr_weight, L0_attn_ttt_lr_bias, L0_attn_learnable_token_idx, L0_attn_post_norm_weight, L0_attn_post_norm_bias, L0_ffn_gate_w, L0_ffn_up_w, L0_ffn_down_w, L0_ffn_gate_s, L0_ffn_up_s, L0_ffn_down_s, L1_attn_W_DKV, L1_attn_b_DKV, L1_attn_W_UK, L1_attn_b_UK, L1_attn_W_UV, L1_attn_b_UV, L1_attn_W_DQ, L1_attn_b_DQ, L1_attn_W_UQ, L1_attn_b_UQ, L1_attn_W_QR, L1_attn_W_KR, L1_attn_W_O, L1_attn_b_O, L1_ffn_gate_up_proj, L1_ffn_down_proj):

    def _L0_attn_ref(hidden_states, position_ids, q_w, k_w, v_w, o_w, W1, b1, ttt_norm_weight, ttt_norm_bias, ttt_lr_weight, ttt_lr_bias, learnable_token_idx, post_norm_weight, post_norm_bias):
        import jax, jax.numpy as jnp
        import numpy as np
        NH, HS, K = (32, 512, 16)
        HD = HS // NH
        B, L = (4, 512)
        EPS = 1e-06

        def _ln(x, gamma, beta):
            mu = x.mean(-1, keepdims=True)
            var = x.var(-1, keepdims=True)
            return gamma * ((x - mu) / jnp.sqrt(var + EPS)) + beta

        def _ln_fused_l2_bwd(x, target, gamma, beta):
            D = x.shape[-1]
            mu = x.mean(-1, keepdims=True)
            std = jnp.sqrt(x.var(-1, keepdims=True) + EPS)
            xh = (x - mu) / std
            gxh = (gamma * xh + beta - target) * gamma
            return (D * gxh - gxh.sum(-1, keepdims=True) - xh * (gxh * xh).sum(-1, keepdims=True)) / (D * std)

        def _forward(hidden_states, q_w, k_w, v_w, o_w, W1, b1, ttt_norm_weight, ttt_norm_bias, ttt_lr_weight, ttt_lr_bias, learnable_token_idx, post_norm_weight, post_norm_bias):
            Bb, Ll, _ = hidden_states.shape
            NM = Ll // K

            def proj_heads(w):
                return (hidden_states @ w.T).reshape(Bb, Ll, NH, HD).transpose(0, 2, 1, 3)
            XQ = proj_heads(q_w).reshape(Bb, NH, NM, K, HD)
            XK = proj_heads(k_w).reshape(Bb, NH, NM, K, HD)
            XV = proj_heads(v_w).reshape(Bb, NH, NM, K, HD)
            X = hidden_states.reshape(Bb, NM, K, HS)
            ttt_lr = jnp.einsum('bnkc,hdc->bhnkd', X, ttt_lr_weight) + ttt_lr_bias.reshape(1, NH, 1, 1, 1)
            ttt_lr_eta = jax.nn.sigmoid(ttt_lr).transpose(0, 1, 2, 4, 3) / HD
            token_idx = jnp.clip(1.0 / jnp.arange(1, K + 1, dtype=jnp.float32) + learnable_token_idx, 0.0, None)
            eta = token_idx.reshape(1, 1, 1, K, 1) * ttt_lr_eta
            ln_w = ttt_norm_weight.reshape(NH, 1, HD)
            ln_b = ttt_norm_bias.reshape(NH, 1, HD)

            def step(carry, x):
                W1_s, b1_s = carry
                xq, xk, xv, eta_mb = x
                Z1 = xk @ W1_s + b1_s
                grad = _ln_fused_l2_bwd(Z1, xv - xk, ln_w, ln_b)
                Attn1 = jnp.tril(xq @ xk.swapaxes(-1, -2))
                b1_bar = b1_s - jnp.tril(eta_mb) @ grad
                Z1_bar = xq @ W1_s - eta_mb * Attn1 @ grad + b1_bar
                last_eta = eta_mb[:, :, -1, :, None]
                W1_new = W1_s - (last_eta * xk).swapaxes(-1, -2) @ grad
                b1_new = b1_s - jnp.sum(last_eta * grad, axis=-2, keepdims=True)
                out = xq + _ln(Z1_bar, ln_w, ln_b)
                return ((W1_new, b1_new), out)
            init = (jnp.tile(W1[None], (Bb, 1, 1, 1)), jnp.tile(b1[None], (Bb, 1, 1, 1)))
            xs = (XQ.transpose(2, 0, 1, 3, 4), XK.transpose(2, 0, 1, 3, 4), XV.transpose(2, 0, 1, 3, 4), eta.transpose(2, 0, 1, 3, 4))
            _, ys = jax.lax.scan(step, init, xs)
            out = ys.transpose(1, 0, 3, 2, 4).reshape(Bb, Ll, HS)
            out = _ln(out, post_norm_weight, post_norm_bias)
            return out @ o_w.T
        del position_ids
        return _forward(hidden_states, q_w, k_w, v_w, o_w, W1, b1, ttt_norm_weight, ttt_norm_bias, ttt_lr_weight, ttt_lr_bias, learnable_token_idx, post_norm_weight, post_norm_bias)

    def _L0_ffn_ref(x, gate_w, up_w, down_w, gate_s, up_s, down_s):
        import jax, jax.numpy as jnp
        import numpy as np
        HIDDEN = 512
        INTER = 1408
        B, S = (2, 512)

        def _ternary(key, shape):
            return jax.random.randint(key, shape, -1, 2).astype(jnp.float32)
        b, s, h = x.shape
        xf = x.reshape(b * s, h)
        g = jnp.einsum('th,ih->ti', xf, gate_w) * gate_s
        u = jnp.einsum('th,ih->ti', xf, up_w) * up_s
        hdn = jax.nn.silu(g) * u
        out = jnp.einsum('ti,hi->th', hdn, down_w) * down_s
        return out.reshape(b, s, -1)

    def _L1_attn_ref(hidden_states, W_DKV, b_DKV, W_UK, b_UK, W_UV, b_UV, W_DQ, b_DQ, W_UQ, b_UQ, W_QR, W_KR, W_O, b_O):
        import jax, jax.numpy as jnp
        import numpy as np
        B, S = (1, 1024)
        HID, H, D = (512, 16, 128)
        KVC, QC, RD = (128, 384, 64)
        THETA = 10000.0

        def _mla_forward(hidden_states, W_DKV, b_DKV, W_UK, b_UK, W_UV, b_UV, W_DQ, b_DQ, W_UQ, b_UQ, W_QR, W_KR, W_O, b_O):
            b, s, _ = hidden_states.shape
            c_kv = hidden_states @ W_DKV + b_DKV
            k = (c_kv @ W_UK + b_UK).reshape(b, s, H, D)
            v = (c_kv @ W_UV + b_UV).reshape(b, s, H, D)
            c_q = hidden_states @ W_DQ + b_DQ
            q = (c_q @ W_UQ + b_UQ).reshape(b, s, H, D)
            half = RD // 2
            inv_freq = 1.0 / THETA ** (jnp.arange(0, RD, 2, dtype=jnp.float32) / RD)
            t = jnp.arange(s, dtype=jnp.float32)
            freqs = t[:, None] * inv_freq[None, :]
            cos = jnp.cos(freqs)[None, :, None, :]
            sin = jnp.sin(freqs)[None, :, None, :]
            q_r = q @ W_QR
            k_r = k @ W_KR

            def rope(x):
                x1, x2 = (x[..., :half], x[..., half:])
                first = x1 * cos - x2 * sin
                return jnp.concatenate([first, jnp.zeros_like(first)], axis=-1)
            q = q.at[..., :RD].set(rope(q_r))
            k = k.at[..., :RD].set(rope(k_r))
            scores = jnp.einsum('bqhd,bkhd->bhqk', q, k) / jnp.sqrt(jnp.float32(D))
            probs = jax.nn.softmax(scores, axis=-1)
            ctx = jnp.einsum('bhqk,bkhd->bqhd', probs, v).reshape(b, s, H * D)
            return ctx @ W_O + b_O
        return _mla_forward(hidden_states, W_DKV, b_DKV, W_UK, b_UK, W_UV, b_UV, W_DQ, b_DQ, W_UQ, b_UQ, W_QR, W_KR, W_O, b_O)

    def _L1_ffn_ref(x, gate_up_proj, down_proj):
        import jax, jax.numpy as jnp
        import numpy as np
        NUM_EXPERTS = 4
        B, N, H = x.shape
        E, _, two_I = gate_up_proj.shape
        I = two_I // 2
        G = N // E
        x4 = x.reshape(B, G, E, H)
        gu = jnp.einsum('bgeh,ehd->bged', x4, gate_up_proj)
        gate, up = (gu[..., :I], gu[..., I:])
        inter = jax.nn.silu(gate) * up
        out = jnp.einsum('bgei,eih->bgeh', inter, down_proj)
        return out.reshape(B, N, H)
    x = L0_attn_hidden_states
    xn = _layernorm(x, axis=-1)
    x = x + _L0_attn_ref(xn, L0_attn_position_ids, L0_attn_q_w, L0_attn_k_w, L0_attn_v_w, L0_attn_o_w, L0_attn_W1, L0_attn_b1, L0_attn_ttt_norm_weight, L0_attn_ttt_norm_bias, L0_attn_ttt_lr_weight, L0_attn_ttt_lr_bias, L0_attn_learnable_token_idx, L0_attn_post_norm_weight, L0_attn_post_norm_bias) + _L0_ffn_ref(xn, L0_ffn_gate_w, L0_ffn_up_w, L0_ffn_down_w, L0_ffn_gate_s, L0_ffn_up_s, L0_ffn_down_s)
    xn = _layernorm(x, axis=-1)
    x = x + _L1_attn_ref(xn, L1_attn_W_DKV, L1_attn_b_DKV, L1_attn_W_UK, L1_attn_b_UK, L1_attn_W_UV, L1_attn_b_UV, L1_attn_W_DQ, L1_attn_b_DQ, L1_attn_W_UQ, L1_attn_b_UQ, L1_attn_W_QR, L1_attn_W_KR, L1_attn_W_O, L1_attn_b_O) + _L1_ffn_ref(xn, L1_ffn_gate_up_proj, L1_ffn_down_proj)
    return x

_drawn_inputs = setup_inputs


def setup_inputs(seed=0):
    import zlib

    import numpy as np

    out = dict(_drawn_inputs(seed))
    spreads = {'L0_attn_b1': (0.0, 0.1),
     'L0_attn_ttt_norm_weight': (1.0, 0.2),
     'L0_attn_ttt_norm_bias': (0.0, 0.1),
     'L0_attn_ttt_lr_bias': (0.0, 0.8),
     'L0_attn_learnable_token_idx': (0.0, 0.1),
     'L0_attn_post_norm_weight': (1.0, 0.2),
     'L0_attn_post_norm_bias': (0.0, 0.309),
     'L1_attn_b_DKV': (0.0, 0.728),
     'L1_attn_b_UK': (0.0, 0.8),
     'L1_attn_b_UV': (0.0, 0.372),
     'L1_attn_b_DQ': (0.0, 0.8),
     'L1_attn_b_UQ': (0.0, 0.8),
     'L1_attn_b_O': (0.0, 0.344)}
    factors = {'L1_attn_W_DKV': 8.0,
     'L1_attn_W_UK': 8.0,
     'L1_attn_W_UV': 4.896,
     'L1_attn_W_DQ': 8.0,
     'L1_attn_W_UQ': 8.0,
     'L1_attn_W_QR': 8.0,
     'L1_attn_W_KR': 8.0,
     'L1_ffn_gate_up_proj': 4.803,
     'L1_ffn_down_proj': 4.796}
    for name, (base, spread) in spreads.items():
        noise = np.random.default_rng([zlib.crc32(name.encode()), seed]).standard_normal(out[name].shape)
        drawn = base * np.exp(spread * noise) if base else spread * noise
        out[name] = jnp.asarray(drawn.astype(out[name].dtype))
    for name, factor in factors.items():
        out[name] = (out[name] * factor).astype(out[name].dtype)
    return out
```

```python
import concourse.bass as bass
from concourse import mybir
from contextlib import ExitStack
import numpy as np

F32 = mybir.dt.float32
F32R = mybir.dt.float32r
ALU = mybir.AluOpType
ACT = mybir.ActivationFunctionType
X_AXIS = mybir.AxisListType.X

P = 128
HID = 512
NF = HID // P
BATCH, SEQ = 4, 512
TOK = BATCH * SEQ
TB = 512
NTB = TOK // TB
LN_EPS = 1e-5

NH, HD, CHUNK = 32, 16, 16
TTT_EPS = 1e-6
NPAIR = SEQ // (2 * CHUNK)
NSTEP = SEQ // CHUNK
SUPER = 128
STEPS_PER_SUPER = SUPER // CHUNK
NSUPER = SEQ // SUPER
PAIRS_PER_SUPER = SUPER // (2 * CHUNK)

INTER = 1408
NI = INTER // P

AH, AD = 16, 128
KVC, QC, RD = 128, 384, 64
NQ = QC // P
HALF = RD // 2
NOPE = AD - RD
NEXP = 4
EI = 512


class Chain:

    def __init__(self, eng, sem):
        self.eng, self.sem, self.n = eng, sem, 0

    def link(self, ins):
        self.n += 1
        ins.then_inc(self.sem, 1)
        self.eng.wait_ge(self.sem, self.n)


def exact_matmul(nc, o, w_hi, w_lo, x_hi, x_lo, start, stop):
    nc.tensor.matmul(o, w_hi, x_hi, start=start, stop=False)
    nc.tensor.matmul(o, w_hi, x_lo, start=False, stop=False)
    return nc.tensor.matmul(o, w_lo, x_hi, start=False, stop=stop)


def bcast_rows(dram, n):
    return bass.AP(dram.tensor, dram.offset, [[0, P], [1, n]])


def build(nc, A, out, stop=99):
    with ExitStack() as outer:
        def sb_in(stack):
            return lambda name, shape, dt=F32: stack.enter_context(nc.sbuf_tensor(name, shape, dt))

        sem = lambda name: outer.enter_context(nc.semaphore(name))
        banks = [outer.enter_context(nc.psum_tensor(f"bank{i}", [P, TB], F32)) for i in range(8)]
        sb = sb_in(outer)
        ones_mean = sb("ones_mean", [P, P])
        eps = sb("eps", [P, 2])
        small = sb("small", [P, 40])
        xf_dram = nc.dram_tensor("xf_scratch", [HID, TOK], F32, kind="Internal").ap()
        x1_dram = nc.dram_tensor("x1_scratch", [HID, TOK], F32, kind="Internal").ap()

        fm = lambda d: d.rearrange("(k p) t -> p k t", p=P)

        def layer_norm(tag, eps_col, src, dst, pe_wait=None, affine=None):
            mean_ready, xc_done, sq_done, var_ready, std_done, rec_done, y_done, own = [
                sem(f"{tag}_{x}") for x in ("mean", "xc", "sq", "var", "std", "rec", "y", "own")]
            with ExitStack() as st:
                s = sb_in(st)
                xc = s(f"{tag}_xc", [P, 2, NF, TB])
                sq = s(f"{tag}_sqs", [P, 2, NF, TB])
                std = s(f"{tag}_stds", [P, 2, TB])
                rec = s(f"{tag}_recs", [P, 2, TB])
                with nc.Block() as block:
                    if pe_wait is not None and pe_wait[0] is not None:
                        block.sync(pe_wait[0])

                    @block.tensor
                    def _(pe):
                        def mean(tb):
                            if pe_wait is not None:
                                pe_wait[1](pe, tb)
                            if tb >= 2:
                                pe.wait_ge(xc_done, NF * (tb - 1))
                            for k in range(NF):
                                ins = nc.tensor.matmul(banks[tb % 2][:], ones_mean[:], src(k, tb),
                                                       start=(k == 0), stop=(k == NF - 1))
                            ins.then_inc(mean_ready, 1)

                        def var(tb):
                            pe.wait_ge(sq_done, NF * (tb + 1))
                            if tb >= 2:
                                pe.wait_ge(std_done, tb - 1)
                            for k in range(NF):
                                ins = nc.tensor.matmul(banks[2 + tb % 2][:], ones_mean[:], sq[:, tb % 2, k, :],
                                                       start=(k == 0), stop=(k == NF - 1))
                            ins.then_inc(var_ready, 1)

                        mean(0)
                        for tb in range(NTB):
                            if tb + 1 < NTB:
                                mean(tb + 1)
                            var(tb)

                    @block.scalar
                    def _(act):
                        for tb in range(NTB + 1):
                            if tb < NTB:
                                for k in range(NF):
                                    act.wait_ge(xc_done, NF * tb + k + 1)
                                    if tb >= 2:
                                        act.wait_ge(var_ready, tb - 1)
                                    nc.scalar.activation(sq[:, tb % 2, k, :], xc[:, tb % 2, k, :],
                                                         ACT.Square).then_inc(sq_done, 1)
                            if tb < NTB:
                                act.wait_ge(var_ready, tb + 1)
                                if tb >= 2:
                                    act.wait_ge(rec_done, tb - 1)
                                nc.scalar.activation(std[:, tb % 2, :], banks[2 + tb % 2][:], ACT.Sqrt,
                                                     bias=eps[:, eps_col:eps_col + 1]).then_inc(std_done, 1)
                            if affine is not None and tb >= 1:
                                w, b = affine
                                for k in range(NF):
                                    act.wait_ge(y_done, NF * (tb - 1) + k + 1)
                                    nc.scalar.activation(dst(k, tb - 1), dst(k, tb - 1), ACT.Identity,
                                                         bias=small[:, b + k:b + k + 1],
                                                         scale=small[:, w + k:w + k + 1]).then_inc(own, 1)

                    @block.vector
                    def _(dve):
                        for tb in range(NTB + 1):
                            if tb < NTB:
                                dve.wait_ge(mean_ready, tb + 1)
                                if tb >= 2:
                                    dve.wait_ge(y_done, NF * (tb - 1))
                                    dve.wait_ge(sq_done, NF * (tb - 1))
                                for k in range(NF):
                                    nc.vector.tensor_tensor(xc[:, tb % 2, k, :], src(k, tb), banks[tb % 2][:],
                                                            ALU.subtract).then_inc(xc_done, 1)
                            if tb >= 1:
                                t = tb - 1
                                dve.wait_ge(std_done, t + 1)
                                nc.vector.reciprocal(rec[:, t % 2, :], std[:, t % 2, :]).then_inc(rec_done, 1)
                                dve.wait_ge(rec_done, t + 1)
                                dve.wait_ge(xc_done, NF * (t + 1))
                                for k in range(NF):
                                    a, b, c = dst(k, t), xc[:, t % 2, k, :], rec[:, t % 2, :]
                                    if len(a.shape) == 3:
                                        b = b.rearrange("p (j e) -> p e j", e=NEXP)
                                        c = c.rearrange("p (j e) -> p e j", e=NEXP)
                                    nc.vector.tensor_tensor(a, b, c, ALU.mult).then_inc(y_done, 1)

        def region():
            st = ExitStack()
            outer.callback(st.close)
            return st

        L0a = region()
        s0 = sb_in(L0a)
        xn = s0("xn", [P, NF, TOK])
        x_in = [sem(f"x_in{t}") for t in range(NTB)]
        small_in, const_done = sem("small_in"), sem("const_done")
        SM = dict(down_s=0, post_w=4, post_b=8, ttt_w=12, ttt_b=16)

        with nc.Block() as block:
            @block.vector
            def _(dve):
                nc.vector.memset(ones_mean[:], 1.0 / HID).then_inc(const_done, 1)
                nc.vector.memset(eps[:, 0:1], LN_EPS).then_inc(const_done, 1)
                nc.vector.memset(eps[:, 1:2], TTT_EPS).then_inc(const_done, 1)

            @block.sync
            def _(sp):
                for name, col in SM.items():
                    sp.dma_start(small[:, col:col + NF], A[name]).then_inc(small_in, 16)
                sp.wait_ge(small_in, 16 * len(SM))

        def load_x(sp):
            for t in range(NTB):
                sp.dma_start(x_sb[:, :, t * TB:(t + 1) * TB], fm(A["xT"])[:, :, t * TB:(t + 1) * TB]).then_inc(x_in[t], 16)
            for w, n in ((gate_w, "gate_wT"), (up_w, "up_wT"), (down_w, "down_wT")):
                sp.dma_start(w[:], fm(A[n])).then_inc(fw_in, 16)

        LW = region()
        s0x = sb_in(LW)
        gate_w = s0x("gate_w", [P, NF, INTER])
        up_w = s0x("up_w", [P, NF, INTER])
        down_w = s0x("down_w", [P, NI, HID])
        fw_in = sem("fw_in")
        L0x = region()
        x_sb = sb_in(L0x)("x_sb", [P, NF, TOK])
        layer_norm("ln0", 0, lambda k, t: x_sb[:, k, t * TB:(t + 1) * TB], lambda k, t: xn[:, k, t * TB:(t + 1) * TB],
                   pe_wait=(load_x, lambda pe, t: pe.wait_ge(x_in[t], 16)))

        L0x.close()
        LW.close()
        with ExitStack() as st:
            s = sb_in(st)
            gate_lo = s("gate_lo", [P, NF, INTER], F32R)
            up_lo = s("up_lo", [P, NF, INTER], F32R)
            down_lo = s("down_lo", [P, NI, HID], F32R)
            sc = s("ffn_scales", [P, 2, NI])
            gate_hi = s("gate_hi", [P, NF, INTER], F32R)
            up_hi = s("up_hi", [P, NF, INTER], F32R)
            down_hi = s("down_hi", [P, NI, HID], F32R)
            xn_hi, xn_lo = s("xn_hi", [P, NF, TB], F32R), s("xn_lo", [P, NF, TB], F32R)
            silu_g = s("silu_g", [P, 2, TB])
            hid = s("hid", [P, 2, TB])
            hid_hi, hid_lo = s("hid_hi", [P, 2, TB], F32R), s("hid_lo", [P, 2, TB], F32R)
            ff_out = s("ff_out", [P, 2, TB])
            x_res = s("x_res", [P, 2, TB])
            cut = lambda i: [(raw[:, :, i * P:(i + 1) * P], hi[:, :, i * P:(i + 1) * P], lo[:, :, i * P:(i + 1) * P])
                             for raw, hi, lo in ((gate_w, gate_hi, gate_lo), (up_w, up_hi, up_lo))] + \
                [(down_w[:, i, :], down_hi[:, i, :], down_lo[:, i, :])]
            fsc_in = sem("fsc_in")
            gate_ready, up_ready, silu_done, hid_done, down_ready, ffo_done, wh_done, wl_done, xh_done, xl_done, hh_done, hl_done = [
                sem(x) for x in ("gate_ready", "up_ready", "silu_done", "hid_done", "down_ready", "ffo_done",
                                 "w_hi_done", "w_lo_done", "x_hi_done", "x_lo_done", "hid_hi_done", "hid_lo_done")]
            xf_out = [sem("xf_out0"), sem("xf_out1")]
            xres_in = [sem("xres_in0"), sem("xres_in1")]
            steps = [(t, i) for t in range(NTB) for i in range(NI)]
            with nc.Block() as block:
                @block.sync
                def _(sp):
                    sp.dma_start(sc[:, 0, :], A["gate_s"]).then_inc(fsc_in, 16)
                    sp.dma_start(sc[:, 1, :], A["up_s"]).then_inc(fsc_in, 16)

                    def load_res(q):
                        t, o = q // NF, q % NF
                        sp.dma_start(x_res[:, q % 2, :], fm(A["xT"])[:, o, t * TB:(t + 1) * TB]).then_inc(xres_in[q % 2], 16)

                    load_res(0)
                    load_res(1)
                    for t in range(NTB):
                        for o in range(NF):
                            q = NF * t + o
                            sp.wait_ge(ffo_done, q + 1)
                            sp.dma_start(fm(xf_dram)[:, o, t * TB:(t + 1) * TB], ff_out[:, q % 2, :]).then_inc(xf_out[q % 2], 16)
                            if q + 2 < NTB * NF:
                                load_res(q + 2)
                    for q in range(2):
                        sp.wait_ge(xf_out[q], 16 * NTB * NF // 2)

                @block.gpsimd
                def _(pool):
                    for i in range(NI):
                        for m, (raw, hi, lo) in enumerate(cut(i)):
                            pool.wait_ge(wh_done, 3 * i + m + 1)
                            nc.gpsimd.tensor_tensor(lo, raw, hi.bitcast(F32), ALU.subtract).then_inc(wl_done, 1)

                @block.tensor
                def _(pe):
                    def down(n):
                        t, i = steps[n]
                        if t == 0:
                            pe.wait_ge(wl_done, 3 * i + 3)
                        pe.wait_ge(hl_done, n + 1)
                        if i == 0 and t > 0:
                            pe.wait_ge(ffo_done, NF * t)
                        for o in range(NF):
                            c = slice(o * P, (o + 1) * P)
                            ins = exact_matmul(nc, banks[4 + o][:], down_hi[:, i, c], down_lo[:, i, c], hid_hi[:, n % 2, :],
                                               hid_lo[:, n % 2, :], start=(i == 0), stop=(i == NI - 1))
                        ins.then_inc(down_ready, 1)

                    for n, (t, i) in enumerate(steps):
                        c = slice(i * P, (i + 1) * P)
                        if i == 0 and n >= 1:
                            down(n - 1)
                        if t == 0:
                            pe.wait_ge(wl_done, 3 * i + 1)
                        if n >= 2:
                            pe.wait_ge(silu_done, n - 1)
                        for k in range(NF):
                            if i == 0:
                                pe.wait_ge(xl_done, NF * t + k + 1)
                            ins = exact_matmul(nc, banks[n % 2][:], gate_hi[:, k, c], gate_lo[:, k, c], xn_hi[:, k, :], xn_lo[:, k, :],
                                               start=(k == 0), stop=(k == NF - 1))
                        ins.then_inc(gate_ready, 1)
                        if t == 0:
                            pe.wait_ge(wl_done, 3 * i + 2)
                        if n >= 2:
                            pe.wait_ge(hid_done, n - 1)
                        for k in range(NF):
                            ins = exact_matmul(nc, banks[2 + n % 2][:], up_hi[:, k, c], up_lo[:, k, c], xn_hi[:, k, :], xn_lo[:, k, :],
                                               start=(k == 0), stop=(k == NF - 1))
                        ins.then_inc(up_ready, 1)
                        if i > 0:
                            down(n - 1)
                    down(len(steps) - 1)

                @block.scalar
                def _(act):
                    def split_weights(i):
                        for raw, hi, lo in cut(i):
                            nc.scalar.activation(hi, raw, ACT.Copy).then_inc(wh_done, 1)

                    def split_x(t, k):
                        if t > 0:
                            act.wait_ge(up_ready, NI * t)
                        nc.scalar.activation(xn_hi[:, k, :], xn[:, k, t * TB:(t + 1) * TB], ACT.Copy).then_inc(xh_done, 1)

                    act.wait_ge(fsc_in, 32)
                    act.wait_ge(fw_in, 48)
                    split_x(0, 0)
                    split_weights(0)
                    for k in range(1, NF):
                        split_x(0, k)
                    for n, (t, i) in enumerate(steps):
                        if t == 0 and i + 1 < NI:
                            split_weights(i + 1)
                        act.wait_ge(gate_ready, n + 1)
                        if n >= 2:
                            act.wait_ge(hid_done, n - 1)
                        nc.scalar.activation(silu_g[:, n % 2, :], banks[n % 2][:], ACT.Silu,
                                             scale=sc[:, 0, i:i + 1]).then_inc(silu_done, 1)
                        if i == NI - 1 and t + 1 < NTB:
                            split_x(t + 1, 0)
                        act.wait_ge(hid_done, n + 1)
                        if n >= 2:
                            act.wait_ge(down_ready, n - 1)
                        nc.scalar.activation(hid_hi[:, n % 2, :], hid[:, n % 2, :], ACT.Copy).then_inc(hh_done, 1)
                        if i == NI - 1 and t + 1 < NTB:
                            for k in range(1, NF):
                                split_x(t + 1, k)

                @block.vector
                def _(dve):
                    def split_x(t, k):
                        dve.wait_ge(xh_done, NF * t + k + 1)
                        nc.vector.tensor_tensor(xn_lo[:, k, :], xn[:, k, t * TB:(t + 1) * TB], xn_hi[:, k, :].bitcast(F32),
                                                ALU.subtract).then_inc(xl_done, 1)

                    def finish(t):
                        dve.wait_ge(down_ready, NI * (t + 1))
                        for o in range(NF):
                            q = NF * t + o
                            dve.wait_ge(xres_in[q % 2], 16 * (q // 2 + 1))
                            if q >= 2:
                                dve.wait_ge(xf_out[q % 2], 16 * (q // 2))
                            nc.vector.scalar_tensor_tensor(
                                out=ff_out[:, q % 2, :], in0=banks[4 + o][:], scalar=small[:, SM["down_s"] + o:SM["down_s"] + o + 1],
                                in1=x_res[:, q % 2, :], op0=ALU.mult, op1=ALU.add).then_inc(ffo_done, 1)

                    dve.wait_ge(fsc_in, 32)
                    for k in range(NF):
                        split_x(0, k)
                    for n, (t, i) in enumerate(steps):
                        if i == 1 and t > 0:
                            finish(t - 1)
                        dve.wait_ge(silu_done, n + 1)
                        dve.wait_ge(up_ready, n + 1)
                        if n >= 2:
                            dve.wait_ge(hl_done, n - 1)
                        nc.vector.scalar_tensor_tensor(
                            out=hid[:, n % 2, :], in0=banks[2 + n % 2][:], scalar=sc[:, 1, i:i + 1],
                            in1=silu_g[:, n % 2, :], op0=ALU.mult, op1=ALU.mult).then_inc(hid_done, 1)
                        dve.wait_ge(hh_done, n + 1)
                        nc.vector.tensor_tensor(hid_lo[:, n % 2, :], hid[:, n % 2, :], hid_hi[:, n % 2, :].bitcast(F32),
                                                ALU.subtract).then_inc(hl_done, 1)
                        if i == NI - 1 and t + 1 < NTB:
                            for k in range(NF):
                                split_x(t + 1, k)
                    finish(NTB - 1)
        if stop == 1:
            return dump(nc, sem, out, xf_dram)

        cst_dram = nc.dram_tensor("cst_scratch", [NPAIR, P, HID], F32, kind="Internal").ap()
        L0b = region()
        s0 = sb_in(L0b)
        q_t = s0("q_t", [P, NF, TOK])
        k_t = s0("k_t", [P, NF, TOK])
        L0c = region()
        s0 = sb_in(L0c)
        k_tok = s0("k_tok", [P, NPAIR, HID])
        lr = s0("lr", [P, 2, NPAIR * NH])
        bd16, bd32, ident, t_mask, w2_row = [s0(n, [P, w]) for n, w in (
            ("bd16", P), ("bd32", P), ("ident", P), ("t_mask", P), ("w2_row", HID))]
        cols = s0("cols", [P, 6])
        ntok15 = s0("ntok15", [P, 1])
        w_rep = s0("w_rep", [P, HID])
        s_sum = s0("s_sum", [P, HID])
        avg16 = s0("avg16", [P, P])
        wacc, zbank, zb, psp = banks[0], banks[1], banks[2:4], banks[4:8]
        hd = lambda ap: ap.rearrange("p (h d) -> p h d", d=HD)
        over_d = lambda ap: ap.unsqueeze(2).broadcast_to([P, NH, HD])
        with ExitStack() as st:
            s = sb_in(st)
            qw, kw, vw = [s(n, [P, NF, HID]) for n in ("qw", "kw", "vw")]
            lrw = s("lrw", [P, NF, NH])
            rows = s("rows", [P, HID + NH + 2 * CHUNK])
            b_row, lrb, tokr, invp = rows[:, 0:HID], rows[:, HID:HID + NH], rows[:, HID + NH:HID + NH + CHUNK], rows[:, HID + NH + CHUNK:]
            w_row = s("w_row", [P, HID])
            same, past = s("same", [P, P]), s("past", [P, P])
            w0 = s("w0", [P, NF, HD])
            cs = s("cst_stage", [P, 2, HID])
            xp = s("x_pair", [P, 2, NF, P])
            xp_done = sem("xp_done")
            of_pair = lambda m, kind: 2 * NTB * NF + 3 * m + ("k", "kv", "lr").index(kind)
            mean_w, mean_b = s("mean_w", [P, NF]), s("mean_b", [P, NH])
            pw_in, pc_in, own_s, tok_done, kmv_done, proj_ready, ev_act, ev_dve, cst_done, lr_done, state_done, winit = [
                sem(x) for x in ("pw_in", "pc_in", "setup_chain", "tok_done", "kmv_done", "proj_ready", "ev_act", "ev_dve",
                                 "cst_done", "lr_done", "state_done", "winit")]
            cst_out = [sem("cst_out0"), sem("cst_out1")]
            jobs = [(kind, g, t, "act" if kind == "K" else "dve") for t in range(NTB) for g in range(NF) for kind in "KQ"]
            jobs += [(kind, m, 0, "act" if kind == "k" else "dve") for m in range(NPAIR) for kind in ("k", "kv", "lr")]
            place = [sum(j[3] == jobs[i][3] for j in jobs[:i + 1]) for i in range(len(jobs))]
            with nc.Block() as block:
                @block.sync
                def _(sp):
                    for w, n in ((kw, "k_wT"), (vw, "v_wT"), (qw, "q_wT"), (lrw, "lr_wT")):
                        sp.dma_start(w[:], fm(A[n])).then_inc(pw_in, 16)
                    small_loads = [(w_row[:], bcast_rows(A["ttt_w_row"], HID)), (b_row, bcast_rows(A["ttt_b_row"], HID)),
                                   (lrb, bcast_rows(A["lr_b"], NH)), (tokr, bcast_rows(A["tok_idx"], CHUNK)),
                                   (invp, bcast_rows(A["inv_pos"], CHUNK)), (same[:], A["same_chunk"]), (past[:], A["past_chunk"]),
                                   (bd16[:], A["bd16"]), (bd32[:], A["bd32"]), (ident[:], A["ident"]), (cols[:], A["cols"]),
                                   (w0[:], A["W1"].rearrange("(g p) d -> p g d", p=P))]
                    for dst, src in small_loads:
                        sp.dma_start(dst, src).then_inc(pc_in, 16)
                    sp.wait_ge(state_done, 1)
                    for b in range(BATCH):
                        sp.dma_start(s_sum[32 * b:32 * b + 1, :], A["b1"].rearrange("(a n) -> a n", a=1)).then_inc(pc_in, 16)
                    for m in range(NPAIR):
                        sp.wait_ge(cst_done, m + 1)
                        sp.dma_start(cst_dram[m], cs[:, m % 2, :]).then_inc(cst_out[m % 2], 16)
                    for i in range(2):
                        sp.wait_ge(cst_out[i], 16 * NPAIR // 2)

                @block.gpsimd
                def _(pool):
                    for m in range(NPAIR):
                        if m >= 2:
                            pool.wait_ge(proj_ready, of_pair(m - 2, "lr") + 1)
                        for k in range(NF):
                            nc.gpsimd.tensor_copy(xp[:, m % 2, k, :].rearrange("p (b l) -> p b l", b=BATCH),
                                                  xn[:, k, :].rearrange("p (b l) -> p b l", b=BATCH)[:, :, 32 * m:32 * m + 32])\
                                .then_inc(xp_done, 1)

                @block.tensor
                def _(pe):
                    pe.wait_ge(pw_in, 64)
                    for j, (kind, g, t, _) in enumerate(jobs):
                        if kind == "k":
                            pe.wait_ge(xp_done, NF * (g + 1))
                        if j >= 8:
                            pe.wait_ge(ev_act if jobs[j - 8][3] == "act" else ev_dve, place[j - 8])
                        if kind == "kv":
                            pe.wait_ge(kmv_done, 1)
                        for k in range(NF):
                            if kind in "KQ":
                                w = kw if kind == "K" else qw
                                lhs, rhs, o = w[:, k, g * P:(g + 1) * P], xn[:, k, t * TB:(t + 1) * TB], banks[j % 8][:]
                            else:
                                w = {"k": kw, "kv": vw, "lr": lrw}[kind]
                                lhs, rhs = xp[:, g % 2, k, :], w[:, k, :]
                                o = banks[j % 8][:, 0:NH] if kind == "lr" else banks[j % 8][:]
                            ins = nc.tensor.matmul(o, lhs, rhs, start=(k == 0), stop=(k == NF - 1))
                        ins.then_inc(proj_ready, 1)
                    pe.wait_ge(ev_act, place[len(jobs) - 3])
                    pe.wait_ge(ev_dve, place[-1])
                    pe.wait_ge(state_done, 3)
                    nc.tensor.matmul(wacc[:], ident[:], w_rep[:], start=True, stop=True, skip_group_check=True).then_inc(winit, 1)

                @block.scalar
                def _(act):
                    act.wait_ge(tok_done, 1)
                    for j, (kind, g, t, e) in enumerate(jobs):
                        if e != "act":
                            continue
                        act.wait_ge(proj_ready, j + 1)
                        if kind == "K":
                            ins = nc.scalar.activation(k_t[:, g, t * TB:(t + 1) * TB], banks[j % 8][:], ACT.Copy)
                        else:
                            ins = nc.scalar.activation(k_tok[:, g, :], banks[j % 8][:], ACT.Copy, scale=ntok15[:])
                        ins.then_inc(ev_act, 1)
                    act.wait_ge(ev_dve, place[-1])
                    nc.scalar.activation(lr[:, 0, :], lr[:, 1, :], ACT.Sigmoid).then_inc(lr_done, 1)

                @block.vector
                def _(dve):
                    ch = Chain(dve, own_s)
                    nc.vector.memset(s_sum[:], 0.0).then_inc(state_done, 1)
                    dve.wait_ge(pc_in, 16 * 16)
                    ch.link(nc.vector.tensor_tensor(tokr, tokr, invp, ALU.add))
                    ch.link(nc.vector.tensor_scalar_max(tokr, tokr, 0.0))
                    nc.vector.tensor_scalar_mul(ntok15[:], tokr[:, CHUNK - 1:CHUNK], -1.0).then_inc(tok_done, 1)
                    dve.wait_ge(tok_done, 1)
                    ch.link(nc.vector.tensor_tensor(
                        same[:].rearrange("p (c i) -> p c i", i=CHUNK), same[:].rearrange("p (c i) -> p c i", i=CHUNK),
                        tokr.unsqueeze(1).broadcast_to([P, P // CHUNK, CHUNK]), ALU.mult))
                    ch.link(nc.vector.tensor_scalar(past[:], past[:], ntok15[:], None, ALU.mult))
                    ch.link(nc.vector.tensor_tensor(t_mask[:], past[:], same[:], ALU.subtract))
                    ch.link(nc.vector.tensor_tensor(w2_row[:], w_row[:], w_row[:], ALU.mult))
                    ch.link(nc.vector.tensor_scalar_mul(avg16[:], bd16[:], 1.0 / HD))
                    ch.link(nc.vector.reduce_sum(mean_w[:], w0[:], axis=X_AXIS))
                    ch.link(nc.vector.scalar_tensor_tensor(out=w0[:], in0=mean_w[:].unsqueeze(2).broadcast_to([P, NF, HD]),
                                                           scalar=-1.0 / HD, in1=w0[:], op0=ALU.mult, op1=ALU.add))
                    for g in range(NF):
                        ch.link(nc.vector.tensor_copy(w_rep[:, g * P:(g + 1) * P].rearrange("p (r d) -> p r d", d=HD),
                                                      w0[:, g, :].unsqueeze(1).broadcast_to([P, 8, HD])))
                    ch.link(nc.vector.reduce_sum(mean_b[:], hd(s_sum[:]), axis=X_AXIS))
                    ch.link(nc.vector.scalar_tensor_tensor(out=hd(s_sum[:]), in0=over_d(mean_b[:]), scalar=-1.0 / HD,
                                                           in1=hd(s_sum[:]), op0=ALU.mult, op1=ALU.add))
                    nc.vector.memset(mean_b[:], 0.0).then_inc(state_done, 2)
                    dve.wait_ge(pw_in, 64)
                    nc.vector.tensor_tensor(vw[:], kw[:], vw[:], ALU.subtract).then_inc(kmv_done, 1)
                    for j, (kind, g, t, e) in enumerate(jobs):
                        if e != "dve":
                            continue
                        dve.wait_ge(proj_ready, j + 1)
                        if kind == "Q":
                            ins = nc.vector.tensor_copy(q_t[:, g, t * TB:(t + 1) * TB], banks[j % 8][:])
                        elif kind == "kv":
                            if g >= 2:
                                dve.wait_ge(cst_out[g % 2], 16 * (g // 2))
                            c = cs[:, g % 2, :]
                            nc.vector.tensor_tensor(c, b_row, banks[j % 8][:], ALU.add).then_inc(ev_dve, 1)
                            dve.wait_ge(ev_dve, place[j])
                            nc.vector.tensor_tensor(c, c, w_row[:], ALU.mult).then_inc(cst_done, 1)
                            continue
                        else:
                            ins = nc.vector.tensor_tensor(lr[:, 1, g * NH:(g + 1) * NH], banks[j % 8][:, 0:NH], lrb, ALU.add)
                        ins.then_inc(ev_dve, 1)
                    dve.wait_ge(lr_done, 1)
                    nc.vector.tensor_scalar(lr[:, 1, :], lr[:, 0, :], cols[:, 1:2], 1.0 / HD, ALU.mult, ALU.mult).then_inc(lr_done, 1)
                    dve.wait_ge(lr_done, 2)
                    nc.vector.tensor_scalar(lr[:, 0, :], lr[:, 0, :], cols[:, 0:1], 1.0 / HD, ALU.mult, ALU.mult).then_inc(lr_done, 1)

        with ExitStack() as st:
            s = sb_in(st)
            grad_j = xn[:, 0, :].rearrange("p (b n) -> p b n", b=BATCH)
            grad_bd = xn[:, 1:3, :].rearrange("p a (c h e d) -> p (a c) h e d", c=BATCH * NF * 2, h=2, e=2)
            pt = xn[:, 3, :].rearrange("p (s i h t) -> p s i h t", s=2, i=4, h=2)
            w_now, w_snap = s("w_now", [P, NF, BATCH, P]), [s(f"w_snap{i}", [P, NF, BATCH, P]) for i in range(2)]
            s_snap = s("s_snap", [P, 2, HID])
            cst = s("cst", [P, 2, HID])
            sqz, xh, gt, gx = [s(n, [P, HID]) for n in ("sqz", "xh", "gt", "gx")]
            t1, t2 = gx, sqz
            sg = s("sg", [P, 2, HID])
            sgp = s("sgp", [P, 2, HID])
            sg_bd = s("sg_bd", [P, BATCH, HID])
            st_v, st_s, st_r, st_f, st_a, st_b, st_m = [s("st_" + n, [P, NH]) for n in "vsrfabm"]
            q_bd = s("q_bd", [P, 2, 2, SUPER])
            o_sq, o_std, o_y = [s(n, [P, TB]) for n in ("o_sq", "o_std", "o_y")]
            names = ("z_ready zsq_done zstd_done sg_done sgbd_dve sgbd_act ssum_done d_done wbd_done snap_done gsum_done qbd_done "
                     "p_ready pt_done c_done gbd_done osq_done ovar_ready ostd_done orec_done oxh_done oy_done oq_done chain zero_done")
            (z_ready, zsq_done, zstd_done, sg_done, sgbd_dve, sgbd_act, ssum_done, d_done, wbd_done, snap_done, gsum_done, qbd_done,
             p_ready, pt_done, c_done, gbd_done, osq_done, ovar_ready, ostd_done, orec_done, oxh_done, oy_done, oq_done, own, zero_done) = [
                sem("ttt_" + x) for x in names.split()]
            cst_in = [sem("cst_in0"), sem("cst_in1")]
            grad_in = [sem("grad_in0"), sem("grad_in1")]
            NPART = NSUPER * NF * BATCH
            parts_of = lambda n: [p for p in (2 * (n - STEPS_PER_SUPER), 2 * (n - STEPS_PER_SUPER) + 1) if 0 <= p < NPART]
            at = lambda p: (p // (NF * BATCH), p // BATCH % NF, p % BATCH)
            span = lambda S, b: slice(b * SEQ + S * SUPER, b * SEQ + (S + 1) * SUPER)
            q_super = lambda S, g: q_t[:, g, :].rearrange("p (b l) -> p b l", b=BATCH)[:, :, S * SUPER:(S + 1) * SUPER]
            LAST = NSTEP + STEPS_PER_SUPER + 2
            w_of = lambda n: w_snap[n // STEPS_PER_SUPER % 2] if n % STEPS_PER_SUPER == 0 else w_now
            def groups_at(n):
                k = n - 1 - STEPS_PER_SUPER
                return [k // 2] if k >= 0 and k % 2 == 1 and k // 2 < NSUPER * NF else []

            LINKS = 15
            vsum_at = lambda n: LINKS * n + 1

            with nc.Block() as block:
                @block.sync
                def _(sp):
                    def load_cst(m):
                        if m >= 2:
                            sp.wait_ge(sg_done, 2 * (m - 1))
                        sp.dma_start(cst[:, m % 2, :], cst_dram[m]).then_inc(cst_in[m % 2], 16)

                    load_cst(0)
                    load_cst(1)
                    for m in range(NPAIR):
                        S = m // PAIRS_PER_SUPER
                        sp.wait_ge(gsum_done, m + 1)
                        if m % PAIRS_PER_SUPER == 0 and S > 0:
                            sp.wait_ge(gbd_done, 2 * S)
                        for b in range(BATCH):
                            r = 32 * (m % PAIRS_PER_SUPER)
                            sp.dma_start(grad_j[r:r + 32, b, :], sgp[32 * b:32 * b + 32, m % 2, :]).then_inc(grad_in[m % 2], 16)
                        if m + 2 < NPAIR:
                            load_cst(m + 2)

                @block.gpsimd
                def _(pool):
                    nc.gpsimd.memset(grad_bd, 0.0).then_inc(zero_done, 1)
                    nc.gpsimd.memset(sg_bd[:], 0.0).then_inc(zero_done, 1)
                    for n in range(LAST):
                        if n < NSTEP and n % 2 == 1:
                            m = n // 2
                            pool.wait_ge(sg_done, n + 1)
                            if m >= 2:
                                pool.wait_ge(grad_in[m % 2], 64 * (m // 2))
                            nc.gpsimd.tensor_tensor(sgp[:, m % 2, :], sg[:, 0, :], sg[:, 1, :], ALU.add).then_inc(gsum_done, 1)
                        for G in groups_at(n):
                            S, g = G // NF, G % NF
                            pool.wait_ge(oy_done, G + 1)
                            dst = q_super(S, g)
                            nc.gpsimd.tensor_tensor(dst, dst, o_y[:].rearrange("p (b l) -> p b l", b=BATCH), ALU.add).then_inc(oq_done, 1)

                @block.tensor
                def _(pe):
                    def z_product(n):
                        m = n // 2
                        if n > 0:
                            pe.wait_ge(ssum_done, n)
                        nc.tensor.matmul(zbank[:], bd32[:], s_sum[:], start=True, stop=False, skip_group_check=True)
                        for g in range(NF):
                            if g % 2 == 0:
                                pe.wait_ge(wbd_done, 2 * n + g // 2 + 1)
                            for b in range(BATCH):
                                ins = nc.tensor.matmul(zbank[32 * b:32 * b + 32, g * P:(g + 1) * P],
                                                       k_t[:, g, b * SEQ + 32 * m:b * SEQ + 32 * m + 32], w_of(n)[:, g, b, :],
                                                       start=False, stop=(g == NF - 1), skip_group_check=True)
                        ins.then_inc(z_ready, 1)

                    def state_update(n):
                        m = n // 2
                        pe.wait_ge(sgbd_dve, 2 * (n + 1))
                        pe.wait_ge(sgbd_act, 2 * (n + 1))
                        for g in range(NF):
                            for i in range(4):
                                c = g * P + 32 * i
                                ins = nc.tensor.matmul(wacc[32 * i:32 * i + 32, g * P:(g + 1) * P],
                                                       k_tok[:, m, c:c + 32], sg_bd[:, :, c:c + 32],
                                                       start=False, stop=True, skip_group_check=True)
                        ins.then_inc(d_done, 1)

                    def scores(p):
                        S, g, b = at(p)
                        pe.wait_ge(qbd_done, 2 * (p + 1))
                        if p >= 1:
                            pe.wait_ge(pt_done, 4 * p)
                        G = p // BATCH
                        if p % BATCH == 1 and G >= 1:
                            pe.wait_ge(ostd_done, G)
                        for i in range(4):
                            r = slice(32 * i, 32 * i + 32)
                            ins = nc.tensor.matmul(psp[i][:, 0:2 * SUPER], k_t[r, g, span(S, b)],
                                                   q_bd[r, p % 2, :, :], start=True, stop=True)
                        ins.then_inc(p_ready, 1)

                    def outputs(p):
                        S, g, b = at(p)
                        G = p // BATCH
                        o = zb[G % 2]
                        if b == 0:
                            if G >= 2:
                                pe.wait_ge(oxh_done, G - 1)
                            for bb in range(BATCH):
                                nc.tensor.matmul(o[:, bb * SUPER:(bb + 1) * SUPER], s_snap[:, S % 2, g * P:(g + 1) * P],
                                                 cols[:, 2 + bb:3 + bb].broadcast_to([P, SUPER]),
                                                 start=(bb == 0), stop=False, skip_group_check=True)
                            for bb in range(BATCH):
                                nc.tensor.matmul(o[:, bb * SUPER:(bb + 1) * SUPER], w_snap[S % 2][:, g, bb, :],
                                                 q_t[:, g, span(S, bb)], start=False, stop=False, skip_group_check=True)
                        if p % (NF * BATCH) == 0:
                            pe.wait_ge(gbd_done, 2 * (S + 1))
                        pe.wait_ge(pt_done, 4 * (p + 1))
                        for i in range(4):
                            for h in range(2):
                                ins = nc.tensor.matmul(o[32 * i:32 * i + 32, b * SUPER:(b + 1) * SUPER],
                                                       grad_bd[:, (b * NF + g) * 4 + i, h, :, :].rearrange("p e d -> p (e d)"),
                                                       pt[:, p % 2, i, h, :], start=False, stop=(h == 1), skip_group_check=True)
                        ins.then_inc(c_done, 1)

                    def variances(G):
                        pe.wait_ge(osq_done, G + 1)
                        pe.wait_ge(pt_done, 4 * min(4 * G + 5, NPART))
                        nc.tensor.matmul(psp[0][:], avg16[:], o_sq[:], start=True, stop=True).then_inc(ovar_ready, 1)

                    pe.wait_ge(zero_done, 2)
                    for n in range(LAST):
                        parts = parts_of(n)
                        before = [p for p in parts_of(n - 1)[1:]]
                        if n < NSTEP:
                            z_product(n)
                        for p in before:
                            outputs(p)
                        for p in parts[:1]:
                            scores(p)
                        if n < NSTEP:
                            state_update(n)
                        for G in groups_at(n):
                            variances(G)
                        for p in parts[:1]:
                            outputs(p)
                        for p in parts[1:]:
                            scores(p)

                @block.scalar
                def _(act):
                    for n in range(LAST):
                        parts = parts_of(n)
                        S = n // STEPS_PER_SUPER
                        if n < NSTEP:
                            act.wait_ge(z_ready, n + 1)
                            nc.scalar.activation(sqz[:], zbank[:], ACT.Square).then_inc(zsq_done, 1)
                        for p in parts:
                            Sp, g, b = at(p)
                            if p >= 2:
                                act.wait_ge(p_ready, p - 1)
                            for h in range(2):
                                nc.scalar.activation(q_bd[:, p % 2, h, :], q_t[:, g, span(Sp, b)], ACT.Copy,
                                                     scale=cols[:, h:h + 1]).then_inc(qbd_done, 1)
                            if n < NSTEP and p == parts[0]:
                                act.wait_ge(own, vsum_at(n))
                                nc.scalar.activation(st_s[:], st_v[:], ACT.Sqrt, bias=eps[:, 1:2], scale=1.0 / HD).then_inc(zstd_done, 1)
                        if n < NSTEP and not parts:
                            act.wait_ge(own, vsum_at(n))
                            nc.scalar.activation(st_s[:], st_v[:], ACT.Sqrt, bias=eps[:, 1:2], scale=1.0 / HD).then_inc(zstd_done, 1)
                        if n % STEPS_PER_SUPER == 0 and 1 <= S <= NSUPER:
                            for i in range(2):
                                act.wait_ge(grad_in[i], 128 * S)
                            if S == 1:
                                act.wait_ge(zero_done, 2)
                            else:
                                act.wait_ge(c_done, NF * BATCH * (S - 1))
                            for h in range(2):
                                nc.scalar.activation(grad_bd[:, :, h, h, :],
                                                     grad_j.rearrange("p b (c h d) -> p (b c) h d", h=2, d=HD)[:, :, h, :],
                                                     ACT.Copy).then_inc(gbd_done, 1)
                        for G in groups_at(n):
                            act.wait_ge(c_done, 4 * (G + 1))
                            nc.scalar.activation(o_sq[:], zb[G % 2][:], ACT.Square).then_inc(osq_done, 1)
                        if n < NSTEP:
                            act.wait_ge(sg_done, n + 1)
                            if n == 0:
                                act.wait_ge(zero_done, 2)
                            for b in (2, 3):
                                r = slice(32 * b, 32 * b + 32)
                                nc.scalar.activation(sg_bd[r, b, :], sg[r, n % 2, :], ACT.Copy).then_inc(sgbd_act, 1)
                        for G in groups_at(n):
                            g = G % NF
                            act.wait_ge(ovar_ready, G + 1)
                            nc.scalar.activation(o_std[:], psp[0][:], ACT.Sqrt, bias=eps[:, 1:2]).then_inc(ostd_done, 1)
                            act.wait_ge(oxh_done, G + 1)
                            nc.scalar.activation(o_y[:], o_y[:], ACT.Identity, scale=small[:, SM["ttt_w"] + g:SM["ttt_w"] + g + 1],
                                                 bias=small[:, SM["ttt_b"] + g:SM["ttt_b"] + g + 1]).then_inc(oy_done, 1)


                @block.vector
                def _(dve):
                    ch = Chain(dve, own)

                    def state_copies(n):
                        S = n // STEPS_PER_SUPER
                        if n > 0:
                            dve.wait_ge(d_done, n)
                        if n % STEPS_PER_SUPER == 0:
                            if S >= 2:
                                dve.wait_ge(c_done, NF * BATCH * (S - 1) - 3)
                            nc.vector.tensor_copy(s_snap[:, S % 2, :], s_sum[:]).then_inc(snap_done, 1)
                        for half in range(2):
                            for g in (2 * half, 2 * half + 1):
                                ins = nc.vector.tensor_tensor(
                                    w_of(n)[:, g, :, :].rearrange("p b (i c) -> p b i c", c=32),
                                    wacc[:, g * P:(g + 1) * P].rearrange("p (b c) -> p b c", b=BATCH).unsqueeze(2).broadcast_to([P, BATCH, 4, 32]),
                                    bd16[:].rearrange("p (i c) -> p i c", c=32).unsqueeze(1).broadcast_to([P, BATCH, 4, 32]), ALU.mult)
                            ins.then_inc(wbd_done, 1)

                    def factors(p):
                        dve.wait_ge(p_ready, p + 1)
                        if p >= 2:
                            dve.wait_ge(c_done, p - 1)
                        for i in range(4):
                            nc.vector.scalar_tensor_tensor(
                                out=pt[:, p % 2, i, :, :], in0=psp[i][:, 0:2 * SUPER].rearrange("p (h t) -> p h t", h=2), scalar=1.0,
                                in1=t_mask[:].unsqueeze(1).broadcast_to([P, 2, SUPER]), op0=ALU.add, op1=ALU.mult).then_inc(pt_done, 1)

                    state_copies(0)
                    for n in range(LAST):
                        parts = parts_of(n)
                        if n < NSTEP:
                            m, x = n // 2, n % 2
                            dve.wait_ge(zsq_done, n + 1)
                            ch.link(nc.vector.reduce_sum(st_v[:], hd(sqz[:]), axis=X_AXIS))
                            assert ch.n == vsum_at(n)
                            dve.wait_ge(zstd_done, n + 1)
                            ch.link(nc.vector.reciprocal(st_r[:], st_s[:]))
                            ch.link(nc.vector.tensor_tensor(hd(xh[:]), hd(zbank[:]), over_d(st_r[:]), ALU.mult))
                            ch.link(nc.vector.tensor_tensor(gt[:], xh[:], w2_row[:], ALU.mult))
                            dve.wait_ge(cst_in[m % 2], 16 * (m // 2 + 1))
                            ch.link(nc.vector.tensor_tensor(gt[:], gt[:], cst[:, m % 2, :], ALU.add))
                            ch.link(nc.vector.tensor_tensor(gx[:], gt[:], xh[:], ALU.mult))
                            ch.link(nc.vector.reduce_sum(st_a[:], hd(gx[:]), axis=X_AXIS))
                            ch.link(nc.vector.reduce_sum(st_b[:], hd(gt[:]), axis=X_AXIS))
                            ch.link(nc.vector.reduce_sum(st_m[:], hd(xh[:]), axis=X_AXIS))
                            ch.link(nc.vector.scalar_tensor_tensor(out=st_m[:], in0=st_a[:], scalar=-1.0 / HD, in1=st_m[:],
                                                                   op0=ALU.mult, op1=ALU.mult))
                            ch.link(nc.vector.tensor_tensor(st_b[:], st_b[:], st_m[:], ALU.add))
                            ch.link(nc.vector.scalar_tensor_tensor(out=hd(t1[:]), in0=over_d(st_a[:]), scalar=-1.0 / HD, in1=hd(xh[:]),
                                                                   op0=ALU.mult, op1=ALU.mult))
                            ch.link(nc.vector.scalar_tensor_tensor(out=hd(t2[:]), in0=over_d(st_b[:]), scalar=-1.0 / HD, in1=hd(gt[:]),
                                                                   op0=ALU.mult, op1=ALU.add))
                            ch.link(nc.vector.tensor_tensor(t1[:], t1[:], t2[:], ALU.add))
                            ch.link(nc.vector.tensor_tensor(st_f[:], st_r[:], lr[:, x, m * NH:(m + 1) * NH], ALU.mult))
                            if n >= 2:
                                dve.wait_ge(gsum_done, m)
                            nc.vector.tensor_tensor(hd(sg[:, x, :]), hd(t1[:]), over_d(st_f[:]), ALU.mult).then_inc(sg_done, 1)
                            dve.wait_ge(sg_done, n + 1)
                            if n == 0:
                                dve.wait_ge(zero_done, 2)
                            for b in (0, 1):
                                r = slice(32 * b, 32 * b + 32)
                                nc.vector.tensor_copy(sg_bd[r, b, :], sg[r, x, :]).then_inc(sgbd_dve, 1)
                            if n == 0:
                                dve.wait_ge(snap_done, 1)
                            elif n % STEPS_PER_SUPER == 0:
                                dve.wait_ge(snap_done, n // STEPS_PER_SUPER + 1)
                            nc.vector.scalar_tensor_tensor(out=s_sum[:], in0=sg[:, x, :], scalar=ntok15[:], in1=s_sum[:],
                                                           op0=ALU.mult, op1=ALU.add).then_inc(ssum_done, 1)
                        for p in parts[:1]:
                            factors(p)
                        if n + 1 < NSTEP:
                            dve.wait_ge(ssum_done, n + 1)
                            state_copies(n + 1)
                        for G in groups_at(n):
                            dve.wait_ge(ostd_done, G + 1)
                            nc.vector.reciprocal(o_std[:], o_std[:]).then_inc(orec_done, 1)
                            dve.wait_ge(orec_done, G + 1)
                            if G >= 1:
                                dve.wait_ge(oq_done, G)
                            nc.vector.tensor_tensor(o_y[:], zb[G % 2][:], o_std[:], ALU.mult).then_inc(oxh_done, 1)
                        for p in parts[1:]:
                            factors(p)
        if stop == 2:
            return dump(nc, sem, out.rearrange("(k p) t -> p k t", p=P), q_t[:])

        L0c.close()

        for_tb = lambda ten: (lambda k, t: ten[:, k, t * TB:(t + 1) * TB])
        LE = region()
        s0x = sb_in(LE)
        gup = s0x("gup", [P, 2, NF, 2 * EI])
        dnp = s0x("dnp", [P, 2, NF, HID])
        ow = s0x("ow", [P, NF, HID])
        ew_in, ow_in = [sem("ew_in0"), sem("ew_in1")], sem("ow_in")

        def load_expert(sp, e):
            sp.dma_start(gup[:, e % 2, :, :], fm(A["gup"][e])).then_inc(ew_in[e % 2], 16)
            sp.dma_start(dnp[:, e % 2, :, :], fm(A["dnp"][e])).then_inc(ew_in[e % 2], 16)

        def load_ahead(sp):
            sp.dma_start(ow[:], fm(A["o_wT"])).then_inc(ow_in, 16)
            load_expert(sp, 0)
            load_expert(sp, 1)

        layer_norm("post", 1, for_tb(q_t), for_tb(q_t), affine=(SM["post_w"], SM["post_b"]), pe_wait=(load_ahead, lambda pe, t: None))
        x1 = k_t
        with ExitStack() as st:
            s = sb_in(st)
            xf = s("xf", [P, 2, NF, TB])
            oproj_ready, x1_done = sem("oproj_ready"), sem("x1_done")
            xf_in = [sem("xf_in0"), sem("xf_in1")]
            with nc.Block() as block:
                @block.sync
                def _(sp):
                    for t in range(NTB):
                        if t >= 2:
                            sp.wait_ge(x1_done, NF * (t - 1))
                        sp.dma_start(xf[:, t % 2, :, :], fm(xf_dram)[:, :, t * TB:(t + 1) * TB]).then_inc(xf_in[t % 2], 16)

                @block.tensor
                def _(pe):
                    pe.wait_ge(ow_in, 16)
                    for j in range(NTB * NF):
                        t, o = j // NF, j % NF
                        if j >= 4:
                            pe.wait_ge(x1_done, j - 3)
                        for k in range(NF):
                            ins = nc.tensor.matmul(banks[j % 4][:], ow[:, k, o * P:(o + 1) * P], q_t[:, k, t * TB:(t + 1) * TB],
                                                   start=(k == 0), stop=(k == NF - 1))
                        ins.then_inc(oproj_ready, 1)

                @block.vector
                def _(dve):
                    for j in range(NTB * NF):
                        t, o = j // NF, j % NF
                        if o == 0:
                            dve.wait_ge(xf_in[t % 2], 16 * (t // 2 + 1))
                        dve.wait_ge(oproj_ready, j + 1)
                        nc.vector.tensor_tensor(x1[:, o, t * TB:(t + 1) * TB], xf[:, t % 2, o, :], banks[j % 4][:], ALU.add)\
                            .then_inc(x1_done, 1)
        layer_norm("ln1", 0, for_tb(x1), lambda k, t: xn[:, k, t * TB:(t + 1) * TB].rearrange("p (e j) -> p e j", e=NEXP))
        if stop == 3:
            return dump(nc, sem, out.rearrange("(k p) t -> p k t", p=P), x1[:])

        w_o = q_t[:].rearrange("p k (a n) -> p (k a) n", n=HID)
        wo_in = sem("wo_in")
        xg_dram = nc.dram_tensor("xg_scratch", [HID, TOK], F32, kind="Internal").ap()
        with ExitStack() as st:
            s = sb_in(st)
            e_silu = s("e_silu", [P, 2, TB])
            e_hid = s("e_hid", [P, 2, 4, TB])
            e_out = s("e_out", [P, 2, TB])
            eg_ready, eu_ready, es_done, eh_done, ed_ready, eo_done = [sem(x) for x in (
                "eg_ready", "eu_ready", "es_done", "eh_done", "ed_ready", "eo_done")]
            xg_out = [sem("xg_out0"), sem("xg_out1")]
            NEI = EI // P
            of_expert = lambda ap, e: ap.rearrange("p (b e j) -> p e b j", b=BATCH, e=NEXP)[:, e, :, :]
            with nc.Block() as block:
                @block.sync
                def _(sp):
                    sp.dma_start(w_o, A["W_O"].rearrange("(h d) n -> d h n", d=AD)).then_inc(wo_in, 16)
                    for e in range(NEXP):
                        for o in range(NF):
                            q = NF * e + o
                            sp.wait_ge(eo_done, q + 1)
                            sp.dma_start(of_expert(fm(xg_dram)[:, o, :], e), e_out[:, q % 2, :].rearrange("p (b j) -> p b j", b=BATCH))\
                                .then_inc(xg_out[q % 2], 16)
                        if e + 2 < NEXP:
                            sp.wait_ge(ed_ready, NF * (e + 1))
                            load_expert(sp, e + 2)
                    for q in range(2):
                        sp.wait_ge(xg_out[q], 16 * NEXP * NF // 2)

                @block.tensor
                def _(pe):
                    for e in range(NEXP):
                        pe.wait_ge(ew_in[e % 2], 32 * (e // 2 + 1))
                        for i in range(NEI):
                            n = NEI * e + i
                            for half, free, ready in ((0, es_done, eg_ready), (1, eh_done, eu_ready)):
                                if n >= 2:
                                    pe.wait_ge(free, n - 1)
                                c = half * EI + i * P
                                for k in range(NF):
                                    ins = nc.tensor.matmul(banks[2 * half + n % 2][:], gup[:, e % 2, k, c:c + P], of_expert(xn[:, k, :], e),
                                                           start=(k == 0), stop=(k == NF - 1))
                                ins.then_inc(ready, 1)
                        pe.wait_ge(eh_done, NEI * (e + 1))
                        for o in range(NF):
                            q = NF * e + o
                            if q >= 4:
                                pe.wait_ge(eo_done, q - 3)
                            for i in range(NEI):
                                ins = nc.tensor.matmul(banks[4 + q % 4][:], dnp[:, e % 2, i, o * P:(o + 1) * P], e_hid[:, e % 2, i, :],
                                                       start=(i == 0), stop=(i == NEI - 1))
                            ins.then_inc(ed_ready, 1)

                @block.scalar
                def _(act):
                    for n in range(NEXP * NEI):
                        act.wait_ge(eg_ready, n + 1)
                        if n >= 2:
                            act.wait_ge(eh_done, n - 1)
                        nc.scalar.activation(e_silu[:, n % 2, :], banks[n % 2][:], ACT.Silu).then_inc(es_done, 1)

                @block.vector
                def _(dve):
                    for e in range(NEXP):
                        for i in range(NEI):
                            n = NEI * e + i
                            dve.wait_ge(es_done, n + 1)
                            dve.wait_ge(eu_ready, n + 1)
                            if e >= 2 and i == 0:
                                dve.wait_ge(ed_ready, NF * (e - 1))
                            nc.vector.tensor_tensor(e_hid[:, e % 2, i, :], e_silu[:, n % 2, :], banks[2 + n % 2][:], ALU.mult)\
                                .then_inc(eh_done, 1)
                        for o in range(NF):
                            q = NF * e + o
                            dve.wait_ge(ed_ready, q + 1)
                            if q >= 2:
                                dve.wait_ge(xg_out[q % 2], 16 * (q // 2))
                            nc.vector.tensor_tensor(e_out[:, q % 2, :].rearrange("p (b j) -> p b j", b=BATCH),
                                                    x1[:, o, :].rearrange("p (b j e) -> p e b j", b=BATCH, e=NEXP)[:, e, :, :],
                                                    banks[4 + q % 4][:].rearrange("p (b j) -> p b j", b=BATCH), ALU.add).then_inc(eo_done, 1)
        LE.close()
        if stop == 4:
            return dump(nc, sem, out, xg_dram)

        s = sb_in(region())
        HG = 4
        NHG = AH // HG
        ckv = s("ckv", [P, TOK])
        cq = s("cq", [P, NQ, TOK])
        ckv_tok = s("ckv_tok", [P, TOK // P, KVC])
        wq = s("wq", [P, NQ, NHG, 4, P])
        wk = s("wk", [P, NHG, 4, P])
        w_uvo = k_t[:].rearrange("p k (a n) -> p (k a) n", n=HID)
        cosin = s("cosin", [P, 2, SEQ])
        id1 = s("id1", [P, P])
        rope_b = s("rope_b", [P, 2, 2, NHG])
        nope_b = s("nope_b", [P, 2, AH // 2])
        bo = s("bo", [P, NF])
        with ExitStack() as st:
            s2 = sb_in(st)
            w_uqt = cq[:].rearrange("p k t -> p (k t)").rearrange("p (h c) -> p h c", c=QC)
            w_uvt = ckv[:].rearrange("p (h c) -> p h c", c=KVC)
            w_ukt = s2("w_ukt", [P, AH, KVC])
            b_uv, b_row, one = s2("b_uv", [P, AH]), s2("b_out_row", [1, HID]), s2("one", [1, 1])
            vo_in, vo_ready, vo_done, one_done = sem("vo_in"), sem("vo_ready"), sem("vo_done"), sem("one_done")
            w_rot = s2("w_rot", [P, 2, RD])
            b_qk = s2("b_qk", [P, 2, AH])
            w_dq, w_dkv = s2("w_dq", [P, NF, QC]), s2("w_dkv", [P, NF, KVC])
            b_lat = s2("b_lat", [P, 1 + NQ])
            b_kv_row = s2("b_kv_row", [P, KVC])
            aw_in, lat_ready, lat_act, lat_dve, = [sem(x) for x in ("aw_in", "lat_ready", "lat_act", "lat_dve")]
            loads = [(w_dkv[:], fm(A["W_DKV"])), (w_dq[:], fm(A["W_DQ"])), (b_lat[:, 0:1], A["b_DKV"]), (b_lat[:, 1:], A["b_DQ"]),
                     (b_kv_row[:], bcast_rows(A["b_DKV_row"], KVC)), (w_rot[:, 0, :], A["W_QR"]), (w_rot[:, 1, :], A["W_KR"]),
                     (b_qk[:, 0, :], A["b_UQ"]), (b_qk[:, 1, :], A["b_UK"]), (cosin[:, 0, :], A["cos"]), (cosin[:, 1, :], A["sin"]),
                     (id1[:], A["ident"]), (nope_b[:, 0, :], A["b_UQ_nope"]), (nope_b[:, 1, :], A["b_UK_nope"]),
                     (w_ukt[:], A["W_UKT"].rearrange("(h d) c -> d h c", d=AD)), (w_uqt, A["W_UQT"].rearrange("(h d) c -> d h c", d=AD))]
            for g in range(NHG):
                for j in range(2):
                    c = (HG * g + 2 * j) * AD
                    two = lambda ap: ap.rearrange("p (h d) -> p h d", d=AD)[:, :, RD:]
                    loads.append((wk[:, g, 2 + j, :].rearrange("p (h d) -> p h d", h=2), two(A["W_UK"][:, c:c + 2 * AD])))
                    for k in range(NQ):
                        loads.append((wq[:, k, g, 2 + j, :].rearrange("p (h d) -> p h d", h=2), two(A["W_UQ"][k * P:(k + 1) * P, c:c + 2 * AD])))
            jobs = [("wk", g, 0, "dve") for g in range(NHG)] + [("wq", g, k, "dve") for g in range(NHG) for k in range(NQ)] + [("bias", 0, 0, "dve")]
            jobs += [("ckv", 0, t, "act") for t in range(NTB)] + [("cq", m, t, "act") for t in range(NTB) for m in range(NQ)]
            jobs += [("tok", m, 0, "dve") for m in range(TOK // P)]
            place = [sum(j[3] == jobs[i][3] for j in jobs[:i + 1]) for i in range(len(jobs))]
            with nc.Block() as block:
                @block.sync
                def _(sp):
                    for dst, src in ((w_uvt, A["W_UVT"].rearrange("(h d) c -> d h c", d=AD)), (b_uv[:], A["b_UV"]), (bo[:], A["b_O"])):
                        sp.dma_start(dst, src).then_inc(vo_in, 16)
                    for dst, src in loads:
                        sp.dma_start(dst, src).then_inc(aw_in, 16)
                    sp.wait_ge(aw_in, 16 * len(loads))

                @block.tensor
                def _(pe):
                    pe.wait_ge(vo_in, 48)
                    pe.wait_ge(wo_in, 16)
                    for h in range(AH):
                        if h >= 4:
                            pe.wait_ge(vo_done, h - 3)
                        nc.tensor.matmul(banks[h % 4][:], w_uvt[:, h, :], w_o[:, h, :], start=True, stop=True).then_inc(vo_ready, 1)
                    for h in range(AH):
                        ins = nc.tensor.matmul(banks[4][0:1, :], b_uv[:, h:h + 1], w_o[:, h, :], start=(h == 0), stop=(h == AH - 1))
                    ins.then_inc(vo_ready, 1)
                    pe.wait_ge(vo_done, AH + 1)
                    pe.wait_ge(one_done, 1)
                    for o in range(NF):
                        ins = nc.tensor.matmul(banks[5][:, o:o + 1], b_row[0:1, o * P:(o + 1) * P], one[:],
                                               start=(o == 0), stop=True, skip_group_check=True)
                    ins.then_inc(vo_ready, 1)
                    pe.wait_ge(vo_done, AH + 2)
                    pe.wait_ge(aw_in, 16 * len(loads))
                    for n, (kind, m, t, _) in enumerate(jobs):
                        bank = banks[n % 8]
                        if n >= 8:
                            pe.wait_ge(lat_act if jobs[n - 8][3] == "act" else lat_dve, place[n - 8])
                        if kind in ("ckv", "cq"):
                            w = w_dkv if kind == "ckv" else w_dq
                            for k in range(NF):
                                ins = nc.tensor.matmul(bank[:], w[:, k, m * P:(m + 1) * P], xn[:, k, t * TB:(t + 1) * TB],
                                                       start=(k == 0), stop=(k == NF - 1))
                        elif kind == "tok":
                            for k in range(NF):
                                ins = nc.tensor.matmul(bank[:, 0:KVC], xn[:, k, m * P:(m + 1) * P], w_dkv[:, k, :],
                                                       start=(k == 0), stop=(k == NF - 1))
                        elif kind == "bias":
                            first = True
                            for qk in range(2):
                                for half in range(2):
                                    for hh in range(HG):
                                        c = (2 * qk + half) * NHG
                                        ins = nc.tensor.matmul(bank[32 * hh:32 * hh + 32, c:c + NHG], w_rot[:, qk, half * HALF:(half + 1) * HALF],
                                                               b_qk[:, qk, :].rearrange("p (g h) -> p h g", h=HG)[:, hh, :],
                                                               start=(qk + half == 0), stop=True, skip_group_check=True)
                        else:
                            for hh in range(HG):
                                h = HG * m + hh
                                lhs = w_ukt[:, h, :] if kind == "wk" else w_uqt[:, h, t * P:(t + 1) * P]
                                ins = nc.tensor.matmul(bank[:, hh * RD:(hh + 1) * RD], lhs, w_rot[:, kind == "wk", :],
                                                       start=(hh == 0), stop=True, skip_group_check=True)
                        ins.then_inc(lat_ready, 1)

                @block.scalar
                def _(act):
                    for n, (kind, m, t, e) in enumerate(jobs):
                        if e == "act":
                            act.wait_ge(lat_ready, n + 1)
                            dst, c = (ckv[:, t * TB:(t + 1) * TB], 0) if kind == "ckv" else (cq[:, m, t * TB:(t + 1) * TB], 1 + m)
                            nc.scalar.activation(dst, banks[n % 8][:], ACT.Identity, bias=b_lat[:, c:c + 1]).then_inc(lat_act, 1)

                @block.vector
                def _(dve):
                    nc.vector.memset(one[:], 1.0).then_inc(one_done, 1)
                    for h in range(AH):
                        dve.wait_ge(vo_ready, h + 1)
                        nc.vector.tensor_copy(w_uvo[:, h, :], banks[h % 4][:]).then_inc(vo_done, 1)
                    dve.wait_ge(vo_ready, AH + 1)
                    nc.vector.tensor_copy(b_row[:], banks[4][0:1, :]).then_inc(vo_done, 1)
                    dve.wait_ge(vo_ready, AH + 2)
                    nc.vector.tensor_tensor(bo[:], bo[:], banks[5][:, 0:NF], ALU.add).then_inc(vo_done, 1)
                    for n, (kind, m, t, e) in enumerate(jobs):
                        if e != "dve":
                            continue
                        dve.wait_ge(lat_ready, n + 1)
                        bank = banks[n % 8]
                        if kind == "tok":
                            ins = nc.vector.tensor_tensor(ckv_tok[:, m, :], b_kv_row[:], bank[:, 0:KVC], ALU.add)
                        elif kind == "bias":
                            ins = nc.vector.tensor_copy(rope_b[:].rearrange("p a b g -> p (a b g)"), bank[:, 0:4 * NHG])
                        else:
                            dst = wk[:, m, 0:2, :] if kind == "wk" else wq[:, t, m, 0:2, :]
                            ins = nc.vector.tensor_copy(dst.rearrange("p a (h r) -> p a h r", h=HG),
                                                        bank[:, 0:HG * RD].rearrange("p (h a r) -> p a h r", h=HG, a=2))
                        ins.then_inc(lat_dve, 1)

        SCALE = float(1.0 / np.sqrt(np.float32(AD)))
        s = sb_in(region())
        ctx_t = xn[:].rearrange("p k (a n) -> p (k a) n", n=SEQ)
        qk = q_t[:].rearrange("p k (b c l) -> p (k b c) l", b=2, c=2).rearrange("p (s a h) l -> p s a h l", s=2, a=2)
        probs = s("probs", [P, 3, SEQ])
        p_t = s("p_t", [P, 2, 4, SEQ])
        rot = s("rot", [P, 2, SEQ])
        xg = s("xg", [P, 2, SEQ])
        nmax, rsum = s("nmax", [P, 4]), s("rsum", [P, 4])
        (pr_ready, rope_ev, rope_done, nope_done, s_ready, max_done, exp_done, norm_done, t_ready, tev_act, tev_dve, pv_ready, pvev_done,
         o_ready, oev_done, own, zeroed) = [sem("att_" + x) for x in (
            "pr_ready rope_ev rope_done nope_done s_ready max_done exp_done norm_done t_ready tev_act tev_dve pv_ready pvev_done "
            "o_ready oev_done chain zeroed").split()]
        xg_in, y_out = [sem("xg_in0"), sem("xg_in1")], [sem("y_out0"), sem("y_out1")]
        NG, NU = BATCH * NHG, BATCH * AH * 4
        UG = HG * 4
        job_at = {0: 0, 1: 1, 3: 2, 4: 3, 6: 4, 7: 5, 9: 6, 10: 7}
        rotated_at = {2 + 6 * pair + hh: (pair, hh) for pair in range(2) for hh in range(HG)}
        KINDS = [(kq, part) for kq in (1, 0) for part in range(4)]
        JOBS = len(KINDS)
        rope_row = lambda hh: 64 if hh % 2 == 0 else 0
        with nc.Block() as block:
            @block.sync
            def _(sp):
                def load(q):
                    b, o = q // NF, q % NF
                    if q >= 2:
                        sp.wait_ge(y_out[q % 2], 16 * (q // 2))
                    sp.dma_start(xg[:, q % 2, :], fm(xg_dram)[:, o, b * SEQ:(b + 1) * SEQ]).then_inc(xg_in[q % 2], 16)

                load(0)
                load(1)
                for q in range(BATCH * NF):
                    b, o = q // NF, q % NF
                    sp.wait_ge(oev_done, q + 1)
                    sp.dma_start(fm(out)[:, o, b * SEQ:(b + 1) * SEQ], xg[:, q % 2, :]).then_inc(y_out[q % 2], 16)
                    if q + 2 < BATCH * NF:
                        load(q + 2)
                for q in range(2):
                    sp.wait_ge(y_out[q], 16 * BATCH * NF // 2)

            @block.gpsimd
            def _(pool):
                nc.gpsimd.memset(qk, 0.0).then_inc(zeroed, 1)

            @block.tensor
            def _(pe):
                def project(G, j):
                    b, g = G // NHG, G % NHG
                    kq, part = KINDS[j]
                    n = G * JOBS + j
                    if n >= 2:
                        pG, pj = (n - 2) // JOBS, (n - 2) % JOBS
                        done = 2 * (pj // 4) + pj % 4 % 2 + 1
                        if pj % 4 < 2:
                            pe.wait_ge(rope_ev, 4 * pG + done)
                        else:
                            pe.wait_ge(nope_done, 2 * (4 * pG + done))
                    bank = banks[6 + n % 2]
                    if kq == 1:
                        ins = nc.tensor.matmul(bank[:], wk[:, g, part, :], ckv[:, b * SEQ:(b + 1) * SEQ], start=True, stop=True)
                    else:
                        for k in range(NQ):
                            ins = nc.tensor.matmul(bank[:], wq[:, k, g, part, :], cq[:, k, b * SEQ:(b + 1) * SEQ],
                                                   start=(k == 0), stop=(k == NQ - 1))
                    ins.then_inc(pr_ready, 1)

                def scores(u):
                    G, hh, qt = u // UG, u // 4 % HG, u % 4
                    if u % UG == 0:
                        pe.wait_ge(rope_done, 2 * HG * (G + 1))
                        pe.wait_ge(nope_done, 8 * (G + 1))
                    if u >= 3:
                        pe.wait_ge(exp_done, u - 2)
                    nc.tensor.matmul(banks[u % 3][:], qk[:, G % 2, 0, hh, qt * P:(qt + 1) * P], qk[:, G % 2, 1, hh, :],
                                     start=True, stop=True).then_inc(s_ready, 1)

                def turn(u):
                    pe.wait_ge(norm_done, u + 1)
                    if u >= 2:
                        pe.wait_ge(tev_dve if u % 2 else tev_act, u // 2)
                    for kt in range(4):
                        ins = nc.tensor.transpose(banks[3 + u % 2][:, kt * P:(kt + 1) * P], probs[:, u % 3, kt * P:(kt + 1) * P], id1[:])
                    ins.then_inc(t_ready, 1)

                def context(H):
                    b = H // AH
                    pe.wait_ge(tev_act, 2 * (H + 1))
                    pe.wait_ge(tev_dve, 2 * (H + 1))
                    if H >= 1:
                        pe.wait_ge(pvev_done, H)
                    if b >= 1:
                        pe.wait_ge(oev_done, NF * b)
                    for kt in range(4):
                        ins = nc.tensor.matmul(banks[5][:], ckv_tok[:, 4 * b + kt, :], p_t[:, H % 2, kt, :], start=(kt == 0), stop=(kt == 3))
                    ins.then_inc(pv_ready, 1)

                def output(b):
                    pe.wait_ge(pvev_done, AH * (b + 1))
                    for o in range(NF):
                        if NF * b + o >= 1:
                            pe.wait_ge(oev_done, NF * b + o)
                        for h in range(AH):
                            ins = nc.tensor.matmul(banks[5][:], w_uvo[:, h, o * P:(o + 1) * P], ctx_t[:, h, :],
                                                   start=(h == 0), stop=(h == AH - 1))
                        ins.then_inc(o_ready, 1)

                for j in range(JOBS):
                    project(0, j)
                scores(0)
                scores(1)
                for u in range(NU + 2):
                    if u + 2 < NU:
                        scores(u + 2)
                    if u < NU:
                        turn(u)
                    if u >= 4 and u % 4 == 0:
                        context(u // 4 - 1)
                    if u >= 64 and u % 64 == 1:
                        output(u // 64 - 1)
                    G = u // UG
                    if u % UG in job_at and G + 1 < NG:
                        project(G + 1, job_at[u % UG])

            @block.scalar
            def _(act):
                def rest(G, j):
                    kq, part = KINDS[j]
                    if part < 2:
                        return
                    g = G % NHG
                    n = G * JOBS + j
                    act.wait_ge(pr_ready, n + 1)
                    if G >= 2:
                        act.wait_ge(s_ready, UG * (G - 1))
                    for e in range(2):
                        r = slice(64 * e, 64 * e + 64)
                        hh = 2 * (part - 2) + e
                        nc.scalar.activation(qk[r, G % 2, kq, hh, :], banks[6 + n % 2][r, :], ACT.Identity,
                                             bias=nope_b[r, kq, 2 * g + part - 2:2 * g + part - 1]).then_inc(nope_done, 1)

                act.wait_ge(zeroed, 1)
                for j in range(JOBS):
                    rest(0, j)

                def exponent(u):
                    act.wait_ge(max_done, u + 1)
                    if u >= 3:
                        act.wait_ge(t_ready, u - 2)
                    nc.scalar.activation(probs[:, u % 3, :], banks[u % 3][:], ACT.Exp, bias=nmax[:, u % 4:u % 4 + 1], scale=SCALE,
                                         accum_out=rsum[:, u % 4:u % 4 + 1]).then_inc(exp_done, 1)

                exponent(0)
                exponent(1)
                for u in range(NU + 2):
                    if u + 2 < NU:
                        exponent(u + 2)
                    if u < NU and u % 2 == 0:
                        H = u // 4
                        act.wait_ge(t_ready, u + 1)
                        if H >= 2:
                            act.wait_ge(pv_ready, H - 1)
                        nc.scalar.activation(p_t[:, H % 2, :, (u % 4) * P:(u % 4 + 1) * P],
                                             banks[3][:].rearrange("p (k q) -> p k q", k=4), ACT.Copy).then_inc(tev_act, 1)
                    if u >= 4 and u % 4 == 0:
                        H = u // 4 - 1
                        act.wait_ge(pv_ready, H + 1)
                        if H % AH == 0 and H > 0:
                            act.wait_ge(o_ready, NF * (H // AH))
                        nc.scalar.activation(ctx_t[:, H % AH, :], banks[5][:], ACT.Copy).then_inc(pvev_done, 1)
                    G = u // UG
                    if u % UG in job_at and G + 1 < NG:
                        rest(G + 1, job_at[u % UG])

            @block.vector
            def _(dve):
                ch = Chain(dve, own)

                def rotary(G, j):
                    kq, part = KINDS[j]
                    if part >= 2:
                        return
                    g = G % NHG
                    n = G * JOBS + j
                    dve.wait_ge(pr_ready, n + 1)
                    if n >= 4:
                        dve.wait_ge(rope_done, HG * (2 * G + j // 4))
                    nc.vector.scalar_tensor_tensor(out=rot[:, part, :], in0=banks[6 + n % 2][:], scalar=rope_b[:, kq, part, g:g + 1],
                                                   in1=cosin[:, part, :], op0=ALU.add, op1=ALU.mult).then_inc(rope_ev, 1)

                def rotated(G, pair, hh):
                    dve.wait_ge(rope_ev, 4 * G + 2 * pair + 2)
                    if G >= 2:
                        dve.wait_ge(s_ready, UG * (G - 1))
                    r, q = slice(32 * hh, 32 * hh + 32), rope_row(hh)
                    nc.vector.tensor_tensor(qk[q:q + 32, G % 2, KINDS[4 * pair][0], hh, :], rot[r, 0, :], rot[r, 1, :], ALU.subtract)\
                        .then_inc(rope_done, 1)

                def maximum(u):
                    dve.wait_ge(s_ready, u + 1)
                    if u >= 4:
                        dve.wait_ge(exp_done, u - 3)
                    c = nmax[:, u % 4:u % 4 + 1]
                    ch.link(nc.vector.reduce_max(c, banks[u % 3][:], axis=X_AXIS))
                    nc.vector.tensor_scalar_mul(c, c, -SCALE).then_inc(max_done, 1)

                dve.wait_ge(zeroed, 1)
                for j in range(JOBS):
                    rotary(0, j)
                    if j % 4 == 1:
                        for hh in range(HG):
                            rotated(0, j // 4, hh)
                maximum(0)
                maximum(1)
                for u in range(NU + 2):
                    if u < NU:
                        dve.wait_ge(exp_done, u + 1)
                        c = rsum[:, u % 4:u % 4 + 1]
                        ch.link(nc.vector.reciprocal(c, c))
                        nc.vector.tensor_scalar(probs[:, u % 3, :], probs[:, u % 3, :], c, None, ALU.mult).then_inc(norm_done, 1)
                    if u + 2 < NU:
                        maximum(u + 2)
                    if u < NU and u % 2 == 1:
                        H = u // 4
                        dve.wait_ge(t_ready, u + 1)
                        if H >= 2:
                            dve.wait_ge(pv_ready, H - 1)
                        nc.vector.tensor_copy(p_t[:, H % 2, :, (u % 4) * P:(u % 4 + 1) * P],
                                              banks[4][:].rearrange("p (k q) -> p k q", k=4)).then_inc(tev_dve, 1)
                    if u >= 64 and u % 64 == 1:
                        b = u // 64 - 1
                        for o in range(NF):
                            q = NF * b + o
                            dve.wait_ge(o_ready, q + 1)
                            dve.wait_ge(xg_in[q % 2], 16 * (q // 2 + 1))
                            nc.vector.scalar_tensor_tensor(out=xg[:, q % 2, :], in0=banks[5][:], scalar=bo[:, o:o + 1], in1=xg[:, q % 2, :],
                                                           op0=ALU.add, op1=ALU.add).then_inc(oev_done, 1)
                    G = u // UG
                    if u % UG in job_at and G + 1 < NG:
                        rotary(G + 1, job_at[u % UG])
                    if u % UG in rotated_at and G + 1 < NG:
                        rotated(G + 1, *rotated_at[u % UG])


def dump(nc, sem, out, src):
    d = sem("dump")
    with nc.Block() as block:
        @block.sync
        def _(sp):
            sp.dma_start(out, src).then_inc(d, 16)
            sp.wait_ge(d, 16)


def shape_constants():
    r, c = np.arange(P)[:, None], np.arange(P)[None, :]
    f = lambda a: np.ascontiguousarray(a, dtype=np.float32)
    cst = {
        "ident": f(r == c),
        "bd16": f(r // HD == c // HD),
        "bd32": f(r // 32 == c // 32),
        "cols": f(np.concatenate([(r % 32) // CHUNK == np.arange(2)[None, :], r // 32 == np.arange(4)[None, :]], 1)),
        "same_chunk": f((r // CHUNK == c // CHUNK) & (r <= c)),
        "past_chunk": f(r // CHUNK < c // CHUNK),
        "inv_pos": f(np.float32(1.0) / np.arange(1, CHUNK + 1, dtype=np.float32)),
    }
    inv_freq = (np.float32(1.0) / np.float32(10000.0) ** (np.arange(0, RD, 2, dtype=np.float32) / np.float32(RD))).astype(np.float32)
    t = np.arange(SEQ, dtype=np.float32).reshape(SEQ // NEXP, NEXP).T.reshape(-1)
    freqs = (inv_freq[:, None] * t[None, :]).astype(np.float32)
    cst["cos"] = f(np.tile(np.cos(freqs.astype(np.float64)), (4, 1)))
    cst["sin"] = f(np.tile(np.sin(freqs.astype(np.float64)), (4, 1)))
    return cst


def layouts(inp):
    a = {n: np.asarray(v) for n, v in inp.items() if n != "L0_attn_position_ids"}
    col = lambda v, w=P: np.ascontiguousarray(v.reshape(-1, w).T)
    T = lambda v: np.ascontiguousarray(v.T)
    L = {
        "xT": T(a["L0_attn_hidden_states"].reshape(TOK, HID)),
        "down_s": col(a["L0_ffn_down_s"]), "gate_s": col(a["L0_ffn_gate_s"]), "up_s": col(a["L0_ffn_up_s"]),
        "post_w": col(a["L0_attn_post_norm_weight"]), "post_b": col(a["L0_attn_post_norm_bias"]),
        "ttt_w": col(a["L0_attn_ttt_norm_weight"]), "ttt_b": col(a["L0_attn_ttt_norm_bias"]),
        "gate_wT": T(a["L0_ffn_gate_w"]), "up_wT": T(a["L0_ffn_up_w"]), "down_wT": T(a["L0_ffn_down_w"]),
        "q_wT": T(a["L0_attn_q_w"]), "k_wT": T(a["L0_attn_k_w"]), "v_wT": T(a["L0_attn_v_w"]), "o_wT": T(a["L0_attn_o_w"]),
        "lr_wT": T(a["L0_attn_ttt_lr_weight"].reshape(NH, HID)), "lr_b": a["L0_attn_ttt_lr_bias"].reshape(NH),
        "W1": a["L0_attn_W1"].reshape(NH * HD, HD), "b1": a["L0_attn_b1"].reshape(NH * HD),
        "ttt_w_row": a["L0_attn_ttt_norm_weight"].reshape(HID), "ttt_b_row": a["L0_attn_ttt_norm_bias"].reshape(HID),
        "tok_idx": a["L0_attn_learnable_token_idx"],
        "W_DKV": a["L1_attn_W_DKV"], "b_DKV": col(a["L1_attn_b_DKV"]), "b_DKV_row": a["L1_attn_b_DKV"],
        "W_UK": a["L1_attn_W_UK"], "W_UKT": T(a["L1_attn_W_UK"]), "b_UK": col(a["L1_attn_b_UK"]),
        "W_UVT": T(a["L1_attn_W_UV"]), "b_UV": col(a["L1_attn_b_UV"]),
        "W_DQ": a["L1_attn_W_DQ"], "b_DQ": col(a["L1_attn_b_DQ"]),
        "W_UQ": a["L1_attn_W_UQ"], "W_UQT": T(a["L1_attn_W_UQ"]), "b_UQ": col(a["L1_attn_b_UQ"]),
        "b_UQ_nope": col(a["L1_attn_b_UQ"].reshape(AH, AD)[:, RD:].reshape(-1)),
        "b_UK_nope": col(a["L1_attn_b_UK"].reshape(AH, AD)[:, RD:].reshape(-1)),
        "W_QR": a["L1_attn_W_QR"], "W_KR": a["L1_attn_W_KR"], "W_O": a["L1_attn_W_O"], "b_O": col(a["L1_attn_b_O"]),
        "gup": a["L1_ffn_gate_up_proj"], "dnp": a["L1_ffn_down_proj"],
    }
    L.update(shape_constants())
    return L


def kernel(**inputs):
    from concourse import bacc
    from concourse.bass_utils import run_bass_kernel_spmd

    nc = bacc.Bacc("TRN2", target_bir_lowering=False, num_devices=1)
    L = layouts(inputs)
    A = {n: nc.dram_tensor(f"in_{n}", v.shape, F32, kind="ExternalInput").ap() for n, v in L.items()}
    out = nc.dram_tensor("out_T", (HID, TOK), F32, kind="ExternalOutput").ap()
    build(nc, A, out)
    r = run_bass_kernel_spmd(nc, [{f"in_{n}": v for n, v in L.items()}], core_ids=[0])
    y = r.results[0]["out_T"].reshape(HID, BATCH, NEXP, SEQ // NEXP)
    return np.ascontiguousarray(y.transpose(1, 3, 2, 0)).reshape(BATCH, SEQ, HID)
```
